# Optimizing a Trainium2 kernel written in Bass

```python
import numpy as np
import jax
import jax.numpy as jnp

def _softmax(x, axis=-1):
    return jax.nn.softmax(x, axis=axis)

def _gelu(x):
    return jax.nn.gelu(x, approximate=True)

def _silu(x):
    return jax.nn.silu(x)

def _sigmoid(x):
    return jax.nn.sigmoid(x)

def _layernorm(x, axis=-1, eps=1e-05):
    m = jnp.mean(x, axis=axis, keepdims=True)
    v = jnp.var(x, axis=axis, keepdims=True)
    return (x - m) / jnp.sqrt(v + eps)

def _scatter_add(tgt, idx, src, axis=0):
    return tgt.at[idx].add(src)

def _segment_sum(src, seg, n):
    return jax.ops.segment_sum(src, seg, n)
kernel_name = 'mk_dlrm_tower_d1_rec_r8_a84aa4'

def setup_inputs(seed: int=0):
    np.random.seed(seed)
    _w = jnp.asarray

    def _rec_inputs():
        import jax
        import jax.numpy as jnp
        _tk = jax.random.key(seed)
        dense_ctx = jax.random.normal(jax.random.fold_in(_tk, 190), (512, 16), jnp.float32)
        ids = jnp.stack([jax.random.randint(jax.random.fold_in(_tk, 200 + f), (512,), 0, v, jnp.int32) for f, v in enumerate([125000, 12500, 125000, 125000, 1000, 1250, 1000, 1000, 12500, 12500, 1250, 1000, 1250, 1000, 12500, 1250, 125000, 125000, 12500, 1250, 125000, 1000, 12500, 12500, 125000, 1000, 1250, 1250, 1250, 1000, 1000, 1000])], axis=1)
        tbl_0 = 0.05 * jax.random.normal(jax.random.fold_in(_tk, 500 + 0), (125000, 32), jnp.float32)
        tbl_1 = 0.05 * jax.random.normal(jax.random.fold_in(_tk, 500 + 1), (12500, 32), jnp.float32)
        tbl_2 = 0.05 * jax.random.normal(jax.random.fold_in(_tk, 500 + 2), (125000, 32), jnp.float32)
        tbl_3 = 0.05 * jax.random.normal(jax.random.fold_in(_tk, 500 + 3), (125000, 32), jnp.float32)
        tbl_4 = 0.05 * jax.random.normal(jax.random.fold_in(_tk, 500 + 4), (1000, 32), jnp.float32)
        tbl_5 = 0.05 * jax.random.normal(jax.random.fold_in(_tk, 500 + 5), (1250, 32), jnp.float32)
        tbl_6 = 0.05 * jax.random.normal(jax.random.fold_in(_tk, 500 + 6), (1000, 32), jnp.float32)
        tbl_7 = 0.05 * jax.random.normal(jax.random.fold_in(_tk, 500 + 7), (1000, 32), jnp.float32)
        tbl_8 = 0.05 * jax.random.normal(jax.random.fold_in(_tk, 500 + 8), (12500, 32), jnp.float32)
        tbl_9 = 0.05 * jax.random.normal(jax.random.fold_in(_tk, 500 + 9), (12500, 32), jnp.float32)
        tbl_10 = 0.05 * jax.random.normal(jax.random.fold_in(_tk, 500 + 10), (1250, 32), jnp.float32)
        tbl_11 = 0.05 * jax.random.normal(jax.random.fold_in(_tk, 500 + 11), (1000, 32), jnp.float32)
        tbl_12 = 0.05 * jax.random.normal(jax.random.fold_in(_tk, 500 + 12), (1250, 32), jnp.float32)
        tbl_13 = 0.05 * jax.random.normal(jax.random.fold_in(_tk, 500 + 13), (1000, 32), jnp.float32)
        tbl_14 = 0.05 * jax.random.normal(jax.random.fold_in(_tk, 500 + 14), (12500, 32), jnp.float32)
        tbl_15 = 0.05 * jax.random.normal(jax.random.fold_in(_tk, 500 + 15), (1250, 32), jnp.float32)
        tbl_16 = 0.05 * jax.random.normal(jax.random.fold_in(_tk, 500 + 16), (125000, 32), jnp.float32)
        tbl_17 = 0.05 * jax.random.normal(jax.random.fold_in(_tk, 500 + 17), (125000, 32), jnp.float32)
        tbl_18 = 0.05 * jax.random.normal(jax.random.fold_in(_tk, 500 + 18), (12500, 32), jnp.float32)
        tbl_19 = 0.05 * jax.random.normal(jax.random.fold_in(_tk, 500 + 19), (1250, 32), jnp.float32)
        tbl_20 = 0.05 * jax.random.normal(jax.random.fold_in(_tk, 500 + 20), (125000, 32), jnp.float32)
        tbl_21 = 0.05 * jax.random.normal(jax.random.fold_in(_tk, 500 + 21), (1000, 32), jnp.float32)
        tbl_22 = 0.05 * jax.random.normal(jax.random.fold_in(_tk, 500 + 22), (12500, 32), jnp.float32)
        tbl_23 = 0.05 * jax.random.normal(jax.random.fold_in(_tk, 500 + 23), (12500, 32), jnp.float32)
        tbl_24 = 0.05 * jax.random.normal(jax.random.fold_in(_tk, 500 + 24), (125000, 32), jnp.float32)
        tbl_25 = 0.05 * jax.random.normal(jax.random.fold_in(_tk, 500 + 25), (1000, 32), jnp.float32)
        tbl_26 = 0.05 * jax.random.normal(jax.random.fold_in(_tk, 500 + 26), (1250, 32), jnp.float32)
        tbl_27 = 0.05 * jax.random.normal(jax.random.fold_in(_tk, 500 + 27), (1250, 32), jnp.float32)
        tbl_28 = 0.05 * jax.random.normal(jax.random.fold_in(_tk, 500 + 28), (1250, 32), jnp.float32)
        tbl_29 = 0.05 * jax.random.normal(jax.random.fold_in(_tk, 500 + 29), (1000, 32), jnp.float32)
        tbl_30 = 0.05 * jax.random.normal(jax.random.fold_in(_tk, 500 + 30), (1000, 32), jnp.float32)
        tbl_31 = 0.05 * jax.random.normal(jax.random.fold_in(_tk, 500 + 31), (1000, 32), jnp.float32)
        _rk = jax.random.fold_in(_tk, 7)
        W_top1 = 0.0606339 * jax.random.normal(jax.random.fold_in(_tk, 801), (272, 512), jnp.float32)
        W_top2 = 0.0441942 * jax.random.normal(jax.random.fold_in(_tk, 802), (512, 256), jnp.float32)
        W_top3 = 0.0625 * jax.random.normal(jax.random.fold_in(_tk, 803), (256, 1), jnp.float32)
        b_top1 = jnp.zeros((512,), jnp.float32)
        b_top2 = jnp.zeros((256,), jnp.float32)
        return (dense_ctx, ids, tbl_0, tbl_1, tbl_2, tbl_3, tbl_4, tbl_5, tbl_6, tbl_7, tbl_8, tbl_9, tbl_10, tbl_11, tbl_12, tbl_13, tbl_14, tbl_15, tbl_16, tbl_17, tbl_18, tbl_19, tbl_20, tbl_21, tbl_22, tbl_23, tbl_24, tbl_25, tbl_26, tbl_27, tbl_28, tbl_29, tbl_30, tbl_31, W_top1, b_top1, W_top2, b_top2, W_top3)
    dense_ctx, ids, tbl_0, tbl_1, tbl_2, tbl_3, tbl_4, tbl_5, tbl_6, tbl_7, tbl_8, tbl_9, tbl_10, tbl_11, tbl_12, tbl_13, tbl_14, tbl_15, tbl_16, tbl_17, tbl_18, tbl_19, tbl_20, tbl_21, tbl_22, tbl_23, tbl_24, tbl_25, tbl_26, tbl_27, tbl_28, tbl_29, tbl_30, tbl_31, W_top1, b_top1, W_top2, b_top2, W_top3 = _rec_inputs()

    def _L0_rec_setup():
        import jax, jax.numpy as jnp
        import numpy as np
        B, F, D = (512, 32, 32)
        LAYER_SIZE = [128, 128]

        def _cin_forward(inputs, filters):
            x0 = inputs
            prev = inputs
            outs = []
            for W in filters:
                z = jnp.einsum('bhd,bmd->bhmd', x0, prev)
                b, h, m, d = z.shape
                z = z.reshape(b, h * m, d)
                cur = jnp.einsum('bpd,pn->bnd', z, W[0])
                cur = jax.nn.relu(cur)
                prev = cur
                outs.append(cur)
            result = jnp.concatenate(outs, axis=1)
            return jnp.sum(result, axis=-1)
        key = jax.random.key(seed)
        k1, k2, k3 = jax.random.split(key, 3)
        inputs = jax.random.normal(k1, (B, F, D), dtype=jnp.float32)
        field_nums = [F] + LAYER_SIZE
        filter_0 = jax.random.normal(k2, (1, field_nums[0] * field_nums[0], field_nums[1]), dtype=jnp.float32) * 0.05
        filter_1 = jax.random.normal(k3, (1, field_nums[0] * field_nums[1], field_nums[2]), dtype=jnp.float32) * 0.05
        return {'inputs': inputs, 'filter_0': filter_0, 'filter_1': filter_1}
    _L0_rec_all = _L0_rec_setup()
    _L0_rec_in = {k: v for k, v in _L0_rec_all.items() if k in ('filter_0', 'filter_1')}
    del _L0_rec_all
    return {'dense_ctx': dense_ctx, 'ids': ids, 'tbl_0': tbl_0, 'tbl_1': tbl_1, 'tbl_2': tbl_2, 'tbl_3': tbl_3, 'tbl_4': tbl_4, 'tbl_5': tbl_5, 'tbl_6': tbl_6, 'tbl_7': tbl_7, 'tbl_8': tbl_8, 'tbl_9': tbl_9, 'tbl_10': tbl_10, 'tbl_11': tbl_11, 'tbl_12': tbl_12, 'tbl_13': tbl_13, 'tbl_14': tbl_14, 'tbl_15': tbl_15, 'tbl_16': tbl_16, 'tbl_17': tbl_17, 'tbl_18': tbl_18, 'tbl_19': tbl_19, 'tbl_20': tbl_20, 'tbl_21': tbl_21, 'tbl_22': tbl_22, 'tbl_23': tbl_23, 'tbl_24': tbl_24, 'tbl_25': tbl_25, 'tbl_26': tbl_26, 'tbl_27': tbl_27, 'tbl_28': tbl_28, 'tbl_29': tbl_29, 'tbl_30': tbl_30, 'tbl_31': tbl_31, 'W_top1': W_top1, 'b_top1': b_top1, 'W_top2': W_top2, 'b_top2': b_top2, 'W_top3': W_top3, 'L0_rec_filter_0': _L0_rec_in['filter_0'], 'L0_rec_filter_1': _L0_rec_in['filter_1']}

def reference(dense_ctx, ids, tbl_0, tbl_1, tbl_2, tbl_3, tbl_4, tbl_5, tbl_6, tbl_7, tbl_8, tbl_9, tbl_10, tbl_11, tbl_12, tbl_13, tbl_14, tbl_15, tbl_16, tbl_17, tbl_18, tbl_19, tbl_20, tbl_21, tbl_22, tbl_23, tbl_24, tbl_25, tbl_26, tbl_27, tbl_28, tbl_29, tbl_30, tbl_31, W_top1, b_top1, W_top2, b_top2, W_top3, L0_rec_filter_0, L0_rec_filter_1):
    import jax
    import jax.numpy as jnp

    def _L0_rec_ref(inputs, filter_0, filter_1):
        import jax, jax.numpy as jnp
        import numpy as np
        B, F, D = (512, 32, 32)
        LAYER_SIZE = [128, 128]

        def _cin_forward(inputs, filters):
            x0 = inputs
            prev = inputs
            outs = []
            for W in filters:
                z = jnp.einsum('bhd,bmd->bhmd', x0, prev)
                b, h, m, d = z.shape
                z = z.reshape(b, h * m, d)
                cur = jnp.einsum('bpd,pn->bnd', z, W[0])
                cur = jax.nn.relu(cur)
                prev = cur
                outs.append(cur)
            result = jnp.concatenate(outs, axis=1)
            return jnp.sum(result, axis=-1)
        return _cin_forward(inputs, (filter_0, filter_1))
    e = jnp.stack([tbl_0[ids[:, 0]], tbl_1[ids[:, 1]], tbl_2[ids[:, 2]], tbl_3[ids[:, 3]], tbl_4[ids[:, 4]], tbl_5[ids[:, 5]], tbl_6[ids[:, 6]], tbl_7[ids[:, 7]], tbl_8[ids[:, 8]], tbl_9[ids[:, 9]], tbl_10[ids[:, 10]], tbl_11[ids[:, 11]], tbl_12[ids[:, 12]], tbl_13[ids[:, 13]], tbl_14[ids[:, 14]], tbl_15[ids[:, 15]], tbl_16[ids[:, 16]], tbl_17[ids[:, 17]], tbl_18[ids[:, 18]], tbl_19[ids[:, 19]], tbl_20[ids[:, 20]], tbl_21[ids[:, 21]], tbl_22[ids[:, 22]], tbl_23[ids[:, 23]], tbl_24[ids[:, 24]], tbl_25[ids[:, 25]], tbl_26[ids[:, 26]], tbl_27[ids[:, 27]], tbl_28[ids[:, 28]], tbl_29[ids[:, 29]], tbl_30[ids[:, 30]], tbl_31[ids[:, 31]]], axis=1)
    z = _L0_rec_ref(e, L0_rec_filter_0, L0_rec_filter_1)
    z = z.reshape(z.shape[0], -1)
    h = jnp.concatenate([z, dense_ctx], axis=1)
    h = jnp.maximum(h @ W_top1 + b_top1, 0.0)
    h = jnp.maximum(h @ W_top2 + b_top2, 0.0)
    y = h @ W_top3
    return y

_drawn_inputs = setup_inputs


def setup_inputs(seed=0):
    import zlib

    import numpy as np

    out = dict(_drawn_inputs(seed))
    spreads = {'b_top1': (0.0, 0.444), 'b_top2': (0.0, 0.428)}
    factors = {'tbl_0': 6.166,
     'tbl_1': 6.499,
     'tbl_2': 6.13,
     'tbl_3': 5.814,
     'tbl_4': 6.361,
     'tbl_5': 6.36,
     'tbl_6': 5.843,
     'tbl_7': 6.016,
     'tbl_8': 5.94,
     'tbl_9': 6.291,
     'tbl_10': 6.097,
     'tbl_11': 6.265,
     'tbl_12': 5.853,
     'tbl_13': 5.848,
     'tbl_14': 6.185,
     'tbl_15': 5.947,
     'tbl_16': 6.602,
     'tbl_17': 6.093,
     'tbl_18': 6.242,
     'tbl_19': 6.286,
     'tbl_20': 5.743,
     'tbl_21': 6.196,
     'tbl_22': 6.09,
     'tbl_23': 6.24,
     'tbl_24': 6.226,
     'tbl_25': 6.135,
     'tbl_26': 6.006,
     'tbl_27': 6.335,
     'tbl_28': 6.204,
     'tbl_29': 6.111,
     'tbl_30': 5.762,
     'tbl_31': 5.755,
     'L0_rec_filter_1': 8.0}
    for name, (base, spread) in spreads.items():
        noise = np.random.default_rng([zlib.crc32(name.encode()), seed]).standard_normal(out[name].shape)
        drawn = base * np.exp(spread * noise) if base else spread * noise
        out[name] = jnp.asarray(drawn.astype(out[name].dtype))
    for name, factor in factors.items():
        out[name] = (out[name] * factor).astype(out[name].dtype)
    return out
```

```python
from contextlib import ExitStack

import numpy as np

import concourse.bass as bass
from concourse import mybir

F32 = mybir.dt.float32
F32R = mybir.dt.float32r
I32 = mybir.dt.int32
ALU = mybir.AluOpType
ACT = mybir.ActivationFunctionType
AX = mybir.AxisListType

B, F, D = 512, 32, 32
N = 128
COLS = 512
CB = COLS // D
CHUNKS = B // CB
GATHERS = CB * F // 128
WRAP = F // 2
GROUPS = 8
SUB = 4
RING = 4
FULL, POOL, VEC = "F", "P", "V"
KIND = "FPPVPPFP"
SPLIT = [g for g in range(GROUPS) if KIND[g] != FULL]
WHOLE = [g for g in range(GROUPS) if KIND[g] == FULL]
BY_POOL = [g for g in range(GROUPS) if KIND[g] == POOL]
BY_VEC = [g for g in range(GROUPS) if KIND[g] == VEC]
H1, H2, DENSE = 512, 256, 16
EARLY = (CHUNKS - 2) * CB


def upto(kinds, g):
    return kinds.index(g) + 1


def build_cin_tower(nc, tables, ids, row_base, dense_t, w0_a, w0_b, w0_a16, w0_b16, w1, w_top1, b_top1,
                    w_top2, b_top2, w_top3, out):
    ctx = ExitStack()
    with ctx:
        def sb(name, shape, dt=F32):
            return ctx.enter_context(nc.sbuf_tensor(name, shape, dt))

        def ps(name, shape):
            return ctx.enter_context(nc.psum_tensor(name, shape, F32))

        def sem(name):
            return ctx.enter_context(nc.semaphore(name))

        x_dram = nc.dram_tensor("x_dram", [CHUNKS, F + WRAP, COLS], F32, kind="Internal").ap()

        idx = sb("idx", [128, CHUNKS * GATHERS], I32)
        base = sb("base", [128, CHUNKS * GATHERS], I32)
        rows = sb("rows", [128, CHUNKS * GATHERS], I32)
        rows_now = sb("rows_now", [128, 2, GATHERS], I32)
        gathered = sb("gathered", [128, 2, GATHERS, D])
        A = sb("A", [128, GROUPS, COLS])
        R = sb("R", [128, 4, COLS])
        X = sb("X", [128, COLS])
        X16 = sb("X16", [WRAP, COLS])
        Bm = sb("Bm", [128, 2, SUB, COLS])
        z1 = sb("z1", [128, 4, COLS])
        z16 = sb("z16", [WRAP, COLS])
        u = sb("u", [128, COLS])
        v = sb("v", [128, COLS])
        z = sb("z", [128, RING, SUB * COLS])
        z_hi = sb("z_hi", [128, RING, SUB * COLS], F32R)
        z_lo = sb("z_lo", [128, RING, SUB * COLS], F32R)
        w0 = sb("w0", [128, 4, N])
        w016 = sb("w016", [WRAP, N])
        w1_full = sb("w1_full", [128, max(len(WHOLE), 1), SUB * N])
        w1_hi = sb("w1_hi", [128, max(len(SPLIT), 1), SUB * N], F32R)
        w1_lo = sb("w1_lo", [128, max(len(SPLIT), 1), SUB * N], F32R)
        s1 = sb("s1", [128, B])
        s2 = sb("s2", [128, B])
        dense = sb("dense", [DENSE, B])
        wt1 = sb("wt1", [128, 2, H1])
        wt1_dense = sb("wt1_dense", [DENSE, H1])
        wt2 = sb("wt2", [128, H1 // 128, H2])
        wt3 = sb("wt3", [128, H2 // 128])
        bt1 = sb("bt1", [128, H1 // 128])
        bt2 = sb("bt2", [128, H2 // 128])
        y = sb("y", [1, B])
        w0_other = z[:, RING - 1, 0:4 * N].rearrange("p (t n) -> p t n", n=N)
        w016_other = z[0:WRAP, RING - 1, 4 * N:5 * N]
        w1_raw = z[:, 0:2, :].rearrange("p r (g n) -> p (r g) n", n=SUB * N)
        h1 = R
        h2 = A[:, 0:2, :]

        A_ps = ps("A_ps", [128, 2, COLS])
        X_ps = ps("X_ps", [128, COLS])
        acc1 = ps("acc1", [128, COLS])
        acc2 = ps("acc2", [128, 2, COLS])
        top = ps("top", [128, 2, COLS])

        ids_in = sem("ids_in")
        w0_in = sem("w0_in")
        w1_in = sem("w1_in")
        tower_in = sem("tower_in")
        rows_ready = sem("rows_ready")
        rows_staged = sem("rows_staged")
        gather_done = [sem(f"gather_done{p}") for p in range(2)]
        x_written = sem("x_written")
        r_loaded = sem("r_loaded")
        a_loaded = [sem(f"a_loaded{h}") for h in range(2)]
        b_loaded = sem("b_loaded")
        w0_summed = sem("w0_summed")
        w1_hi_ready = sem("w1_hi_ready")
        w1_lo_ready = sem("w1_lo_ready")
        x_copied = sem("x_copied")
        a_copied = sem("a_copied")
        z1_ready = sem("z1_ready")
        l1_done = sem("l1_done")
        u_ready = sem("u_ready")
        s1_ready = sem("s1_ready")
        z_ready = sem("z_ready")
        z_hi_ready = sem("z_hi_ready")
        z_lo_pool = sem("z_lo_pool")
        z_lo_vec = sem("z_lo_vec")
        mm_done = sem("mm_done")
        v_ready = sem("v_ready")
        s2_ready = sem("s2_ready")
        top_done = sem("top_done")
        h_ready = sem("h_ready")
        y_ready = sem("y_ready")
        out_written = sem("out_written")

        def wait_count(eng, s, count):
            if not (isinstance(count, int) and count <= 0):
                eng.wait_ge(s, count)

        def steps(eng, step):
            step(0, 0, 0)
            step(1, 0, 1)
            with eng.Fori(1, CHUNKS // 2 - 2) as i:
                for p in range(2):
                    step(2 * i + p, i, p)
            for c in range(CHUNKS - 4, CHUNKS):
                step(c, c // 2, c % 2)

        def exists(c, ahead):
            return not isinstance(c, int) or c + ahead < CHUNKS

        units = [(1, m) for m in range(H1 // 128)] + [(2, m) for m in range(H2 // 128)] + [(3, 0)]
        U = len(units)

        block = ctx.enter_context(nc.Block())

        @block.sync
        def _(sp):
            def write_x(n_half, q):
                sp.wait_ge(gather_done[q], 16 * GATHERS * (n_half + 1))
                n = 2 * n_half + q
                src = gathered[:, q, :, :].rearrange("p j d -> p (j d)")
                sp.dma_start(x_dram[n, 0:F, :].rearrange("f (s c) -> (f s) c", s=4), src)\
                    .then_inc(x_written, 16)
                sp.dma_start(x_dram[n, F:F + WRAP, :].rearrange("f (s c) -> (f s) c", s=4), src[0:4 * WRAP, :])\
                    .then_inc(x_written, 16)

            def load_r(n_half, q):
                n = 2 * n_half + q
                wait_count(sp, z1_ready, 2 * n)
                wait_count(sp, x_copied, 2 * n)
                sp.wait_ge(x_written, 32 * (n + 1))
                x = x_dram[n, :, :]
                for k in range(4):
                    rot = bass.AP(tensor=x.tensor, offset=x.offset + 4 * k * COLS, ap=[[COLS, F], [1, 4 * COLS]],
                                  runtime_checks=x.runtime_checks)
                    sp.dma_start(R[F * k:F * k + F, :, :].rearrange("p t c -> p (t c)"), rot).then_inc(r_loaded, 16)
                    sp.dma_start(X[F * k:F * k + F, :], x[0:F, :]).then_inc(r_loaded, 16)
                sp.dma_start(X16[:, :], x[WRAP:2 * WRAP, :]).then_inc(r_loaded, 16)

            def load_a(n, half):
                for k in range(4):
                    g0 = half * GROUPS // 2
                    src = x_dram[n, 8 * k + g0:8 * k + g0 + GROUPS // 2, :].rearrange("f c -> (f c)")
                    sp.dma_start(A[32 * k:32 * k + 32, g0:g0 + GROUPS // 2, :].rearrange("p g c -> p (g c)"),
                                 src.partition_broadcast(32)).then_inc(a_loaded[half], 16)

            def load_b(p):
                for j in range(SUB):
                    for k in range(4):
                        sp.dma_start(Bm[32 * k:32 * k + 32, p, j, :], u[32 * j:32 * j + 32, :]).then_inc(b_loaded, 16)

            sp.dma_start(idx[:, :], ids).then_inc(ids_in, 16)
            sp.dma_start(base[:, :], row_base).then_inc(ids_in, 16)
            sp.dma_start(w0[:, :, :], w0_a).then_inc(w0_in, 16)
            sp.dma_start(w016[:, :], w0_a16).then_inc(w0_in, 16)
            sp.dma_start(w0_other, w0_b).then_inc(w0_in, 16)
            sp.dma_start(w016_other, w0_b16).then_inc(w0_in, 16)
            for n, g in enumerate(SPLIT):
                sp.dma_start(w1_raw[:, n, :], w1[:, g, :]).then_inc(w1_in, 16)
            for n, g in enumerate(WHOLE):
                sp.dma_start(w1_full[:, n, :], w1[:, g, :]).then_inc(w1_in, 16)
            write_x(0, 0)
            load_r(0, 0)
            load_a(0, 0)
            load_a(0, 1)
            for dst, src in ((wt1[:, :, :], w_top1[0:2 * N, :].rearrange("(k p) n -> p k n", p=128)),
                             (wt1_dense[:, :], w_top1[2 * N:2 * N + DENSE, :]),
                             (wt2[:, :, :], w_top2.rearrange("(k p) n -> p k n", p=128)),
                             (wt3[:, :], w_top3), (bt1[:, :], b_top1), (bt2[:, :], b_top2), (dense[:, :], dense_t)):
                sp.dma_start(dst, src).then_inc(tower_in, 16)
            write_x(0, 1)
            load_r(0, 1)
            sp.wait_ge(u_ready, 1)
            load_b(0)

            def step(c, i, p):
                if exists(c, 2):
                    write_x(i + 1, p)
                    load_r(i + 1, p)
                if exists(c, 1):
                    sp.wait_ge(a_copied, GROUPS * c + GROUPS // 2)
                    load_a(c + 1, 0)
                    sp.wait_ge(u_ready, c + 2)
                    wait_count(sp, z_ready, GROUPS * c)
                    load_b(1 - p)
                    sp.wait_ge(a_copied, GROUPS * c + GROUPS)
                    load_a(c + 1, 1)

            steps(sp, step)
            sp.wait_ge(y_ready, 2)
            sp.dma_start(out.rearrange("b o -> o b"), y[:, :]).then_inc(out_written, 16)
            sp.wait_ge(out_written, 16)

        @block.gpsimd
        def _(pool):
            def stage_rows(n_half, q):
                n = 2 * n_half + q
                wait_count(pool, x_written, 32 * (n - 1))
                pool.tensor_copy(rows_now[:, q, :], rows[:, bass.ds(GATHERS * n, GATHERS)]).then_inc(rows_staged, 1)
                pool.wait_ge(rows_staged, n + 1)

            def gather(q, j):
                pool.indirect_dma_start(gathered[:, q, j, :], None, tables,
                                        bass.IndirectOffsetOnAxis(ap=rows_now[:, q, j:j + 1], axis=0))\
                    .then_inc(gather_done[q], 16)

            pool.wait_ge(ids_in, 32)
            pool.tensor_tensor(rows[:, :], idx[:, :], base[:, :], ALU.add).then_inc(rows_ready, 1)
            pool.wait_ge(rows_ready, 1)
            for n_half, q in ((0, 0), (0, 1), (1, 0)):
                stage_rows(n_half, q)
                for j in range(GATHERS):
                    gather(q, j)

            def step(c, i, p):
                n_half, q = i + 1 + p, 1 - p
                if exists(c, 3):
                    stage_rows(n_half, q)
                for n in range(max(GATHERS, len(BY_POOL))):
                    if n < len(BY_POOL):
                        g = BY_POOL[n]
                        pool.wait_ge(z_hi_ready, len(SPLIT) * c + upto(SPLIT, g))
                        wait_count(pool, mm_done, GROUPS * c + g - RING + 1)
                        pool.tensor_tensor(z_lo[:, g % RING, :], z[:, g % RING, :], z_hi[:, g % RING, :].bitcast(F32),
                                           ALU.subtract).then_inc(z_lo_pool, 1)
                    if n < GATHERS and exists(c, 3):
                        gather(q, n)

            steps(pool, step)

        @block.scalar
        def _(act):
            def copy_x(c):
                act.wait_ge(r_loaded, 144 * (c + 1))
                wait_count(act, z1_ready, 2 * c)
                act.activation(X_ps[:, :], X[:, :], ACT.Copy).then_inc(x_copied, 2)

            def relu_u(c):
                act.wait_ge(l1_done, c + 1)
                wait_count(act, b_loaded, 256 * c)
                wait_count(act, s1_ready, c)
                act.activation(u[:, :], acc1[:, :], ACT.Relu).then_inc(u_ready, 1)

            def relu_v(c, p):
                act.wait_ge(mm_done, GROUPS * (c + 1))
                wait_count(act, s2_ready, c)
                act.activation(v[:, :], acc2[:, p, :], ACT.Relu).then_inc(v_ready, 1)

            def copy_a(c, g):
                act.wait_ge(a_loaded[g // (GROUPS // 2)], 64 * (c + 1))
                wait_count(act, z_ready, GROUPS * c + g - 1)
                act.activation(A_ps[:, g % 2, :], A[:, g, :], ACT.Copy).then_inc(a_copied, 1)

            def unit_out(n, b0, b1, count):
                layer, m = units[n]
                act.wait_ge(top_done, count)
                src = top[:, n % 2, 0:b1 - b0]
                if layer == 1:
                    act.activation(h1[:, m, b0:b1], src, ACT.Relu, bias=bt1[:, m:m + 1]).then_inc(h_ready, 1)
                elif layer == 2:
                    act.activation(h2[:, m, b0:b1], src, ACT.Relu, bias=bt2[:, m:m + 1]).then_inc(h_ready, 1)
                else:
                    act.activation(y[:, b0:b1], src[0:1, :], ACT.Copy).then_inc(y_ready, 1)

            act.wait_ge(w1_in, 16 * GROUPS)
            for n in range(len(SPLIT)):
                act.activation(w1_hi[:, n, :], w1_raw[:, n, :], ACT.Copy).then_inc(w1_hi_ready, 1)
            copy_x(0)
            relu_u(0)
            copy_x(1)
            copy_a(0, 0)

            def step(c, i, p):
                last = isinstance(c, int) and c == CHUNKS - 1
                for g in range(GROUPS):
                    if g + 1 < GROUPS:
                        copy_a(c, g + 1)
                    elif exists(c, 1):
                        copy_a(c + 1, 0)
                    if g in SPLIT:
                        act.wait_ge(z_ready, GROUPS * c + g + 1)
                        wait_count(act, mm_done, GROUPS * c + g - RING + 1)
                        act.activation(z_hi[:, g % RING, :], z[:, g % RING, :], ACT.Copy).then_inc(z_hi_ready, 1)
                    if g == 1 and not (isinstance(c, int) and c == 0):
                        relu_v(c - 1, 1 - p)
                    if g == 3 and exists(c, 1):
                        relu_u(c + 1)
                    if g == 6 and exists(c, 2):
                        copy_x(c + 2)

            steps(act, step)
            act.wait_ge(tower_in, 16 * 7)
            for n in range(U):
                unit_out(n, 0, EARLY, n + 1)
            relu_v(CHUNKS - 1, 1)
            for n in range(U):
                unit_out(n, EARLY, B, U + n + 1)

        @block.vector
        def _(dve):
            def layer1_products(c):
                dve.wait_ge(x_copied, 2 * (c + 1))
                dve.wait_ge(r_loaded, 144 * (c + 1))
                wait_count(dve, l1_done, c)
                dve.tensor_tensor(z1[:, :, :], X_ps[:, :].unsqueeze(1).to_broadcast([128, 4, COLS]), R[:, :, :],
                                  ALU.mult).then_inc(z1_ready, 1)
                dve.tensor_tensor(z16[:, :], X_ps[0:WRAP, :], X16[:, :], ALU.mult).then_inc(z1_ready, 1)

            def sum_u(c):
                dve.wait_ge(u_ready, c + 1)
                dve.tensor_reduce(s1[:, bass.ds(CB * c, CB)], u[:, :].rearrange("p (b d) -> p b d", d=D), AX.X, ALU.add)\
                    .then_inc(s1_ready, 1)

            def sum_v(c):
                dve.wait_ge(v_ready, c + 1)
                dve.tensor_reduce(s2[:, bass.ds(CB * c, CB)], v[:, :].rearrange("p (b d) -> p b d", d=D), AX.X, ALU.add)\
                    .then_inc(s2_ready, 1)

            def wait_slot_free(c, g):
                before, cc = (g - RING, c) if g >= RING else (g - RING + GROUPS, c - 1)
                if before in WHOLE:
                    wait_count(dve, mm_done, GROUPS * cc + before + 1)
                elif before in BY_POOL:
                    wait_count(dve, z_lo_pool, len(BY_POOL) * cc + upto(BY_POOL, before))
                else:
                    wait_count(dve, z_lo_vec, len(BY_VEC) * cc + upto(BY_VEC, before))

            def low_part(c, g):
                dve.wait_ge(z_hi_ready, len(SPLIT) * c + upto(SPLIT, g))
                wait_count(dve, mm_done, GROUPS * c + g - RING + 1)
                dve.tensor_tensor(z_lo[:, g % RING, :], z[:, g % RING, :], z_hi[:, g % RING, :].bitcast(F32),
                                  ALU.subtract).then_inc(z_lo_vec, 1)

            dve.wait_ge(w0_in, 64)
            for t in range(1, 4):
                dve.tensor_tensor(w0[:, t, :], w0[:, t, :], w0_other[:, t, :], ALU.add)
            for k in range(1, 4):
                dve.tensor_tensor(w0[F * k:F * k + F, 0, :], w0[F * k:F * k + F, 0, :],
                                  w0_other[F * k:F * k + F, 0, :], ALU.add)
            dve.tensor_tensor(w016[:, :], w016[:, :], w016_other, ALU.add).then_inc(w0_summed, 1)
            layer1_products(0)
            dve.wait_ge(w1_hi_ready, len(SPLIT))
            for n in range(len(SPLIT)):
                dve.tensor_tensor(w1_lo[:, n, :], w1_raw[:, n, :], w1_hi[:, n, :].bitcast(F32), ALU.subtract)\
                    .then_inc(w1_lo_ready, 1)
            sum_u(0)
            wait_count(dve, w1_lo_ready, len(SPLIT))
            dve.wait_ge(w0_summed, 1)

            def step(c, i, p):
                if exists(c, 1):
                    layer1_products(c + 1)
                dve.wait_ge(b_loaded, 256 * (c + 1))
                for g in range(GROUPS):
                    dve.wait_ge(a_copied, GROUPS * c + g + 1)
                    wait_slot_free(c, g)
                    dve.tensor_tensor(z[:, g % RING, :].rearrange("p (j c) -> p j c", c=COLS),
                                      A_ps[:, g % 2, :].unsqueeze(1).to_broadcast([128, SUB, COLS]),
                                      Bm[:, p, :, :], ALU.mult).then_inc(z_ready, 1)
                    if g - 1 in BY_VEC:
                        low_part(c, g - 1)
                    if g == 3 and not (isinstance(c, int) and c == 0):
                        sum_v(c - 1)
                    if g == 5 and exists(c, 1):
                        sum_u(c + 1)
                if GROUPS - 1 in BY_VEC:
                    low_part(c, GROUPS - 1)

            steps(dve, step)
            sum_v(CHUNKS - 1)

        @block.tensor
        def _(pe):
            def layer1(c):
                pe.wait_ge(z1_ready, 2 * (c + 1))
                wait_count(pe, u_ready, c)
                for t in range(4):
                    pe.matmul(acc1[:, :], w0[:, t, :], z1[:, t, :], start=(t == 0), stop=False)
                pe.matmul(acc1[:, :], w016[:, :], z16[:, :], start=False, stop=True).then_inc(l1_done, 1)

            def group(c, g, p):
                acc = acc2[:, p, :]
                last = g == GROUPS - 1
                if g in WHOLE:
                    pe.wait_ge(z_ready, GROUPS * c + g + 1)
                    w, n = w1_full, WHOLE.index(g)
                    for j in range(SUB):
                        mm = pe.matmul(acc, w[:, n, N * j:N * j + N], z[:, g % RING, COLS * j:COLS * j + COLS],
                                       start=(g == 0 and j == 0), stop=(last and j == SUB - 1))
                    mm.then_inc(mm_done, 1)
                    return
                n = SPLIT.index(g)
                pe.wait_ge(z_hi_ready, len(SPLIT) * c + n + 1)
                for j in range(SUB):
                    for w in (w1_hi, w1_lo):
                        pe.matmul(acc, w[:, n, N * j:N * j + N], z_hi[:, g % RING, COLS * j:COLS * j + COLS],
                                  start=(g == 0 and j == 0 and w is w1_hi), stop=False)
                if g in BY_POOL:
                    pe.wait_ge(z_lo_pool, len(BY_POOL) * c + upto(BY_POOL, g))
                else:
                    pe.wait_ge(z_lo_vec, len(BY_VEC) * c + upto(BY_VEC, g))
                for j in range(SUB):
                    mm = pe.matmul(acc, w1_hi[:, n, N * j:N * j + N], z_lo[:, g % RING, COLS * j:COLS * j + COLS],
                                   start=False, stop=(last and j == SUB - 1))
                mm.then_inc(mm_done, 1)

            def unit(n, b0, b1, h_before):
                layer, m = units[n]
                M = 1 if layer == 3 else 128
                dst = top[0:M, n % 2, 0:b1 - b0]
                if layer == 1:
                    wait_count(pe, h_ready, h_before + n - 1)
                    terms = [(wt1[:, 0, 128 * m:128 * m + 128], s1[:, b0:b1]), (wt1[:, 1, 128 * m:128 * m + 128], s2[:, b0:b1]),
                             (wt1_dense[:, 128 * m:128 * m + 128], dense[:, b0:b1])]
                elif layer == 2:
                    pe.wait_ge(h_ready, h_before + (H1 // 128 if m == 0 else n - 1))
                    terms = [(wt2[:, k, 128 * m:128 * m + 128], h1[:, k, b0:b1]) for k in range(H1 // 128)]
                else:
                    pe.wait_ge(h_ready, h_before + n)
                    terms = [(wt3[:, k:k + 1], h2[:, k, b0:b1]) for k in range(H2 // 128)]
                for k, (w, rhs) in enumerate(terms):
                    mm = pe.matmul(dst, w, rhs, start=(k == 0), stop=(k == len(terms) - 1))
                mm.then_inc(top_done, 1)

            pe.wait_ge(w0_summed, 1)
            layer1(0)
            pe.wait_ge(w1_in, 16 * GROUPS)
            wait_count(pe, w1_lo_ready, len(SPLIT))

            def step(c, i, p):
                wait_count(pe, v_ready, c - 1)
                for g in range(GROUPS):
                    group(c, g, p)
                    if g == 0 and exists(c, 1):
                        layer1(c + 1)

            steps(pe, step)
            pe.wait_ge(tower_in, 16 * 7)
            pe.wait_ge(s2_ready, CHUNKS - 1)
            pe.wait_ge(s1_ready, CHUNKS)
            for n in range(U):
                unit(n, 0, EARLY, 0)
            pe.wait_ge(s2_ready, CHUNKS)
            pe.wait_ge(y_ready, 1)
            for n in range(U):
                unit(n, EARLY, B, U - 1)


_TABLES = [f"tbl_{f}" for f in range(F)]


def kernel(**inputs):
    import concourse.bacc as bacc
    from concourse.bass_utils import run_bass_kernel_spmd

    tables = np.concatenate([np.asarray(inputs[t]) for t in _TABLES], axis=0)
    sizes = [np.asarray(inputs[t]).shape[0] for t in _TABLES]
    starts = np.array([sum(sizes[:f]) for f in range(F)], np.int32)
    ids = np.asarray(inputs["ids"]).T.reshape(F, CHUNKS, 4, GATHERS).transpose(0, 2, 1, 3).reshape(128, -1)
    row_base = np.broadcast_to(starts[:, None, None], (F, 4, CHUNKS * GATHERS)).reshape(128, -1)
    w0 = np.asarray(inputs["L0_rec_filter_0"])[0].reshape(F, F, N)
    h = np.arange(F)
    first = np.tile(h[None, :, None], (4, 1, 4))
    other = (first + 4 * np.arange(4)[:, None, None] + np.arange(4)) % F
    half = np.arange(WRAP)
    w1 = np.asarray(inputs["L0_rec_filter_1"])[0].reshape(4, GROUPS, SUB, 32, N).transpose(0, 3, 1, 2, 4)
    columns = lambda a, n: np.asarray(a).reshape(n, 128).T
    arrays = {
        "tables": tables,
        "ids": ids,
        "row_base": row_base,
        "dense_t": np.asarray(inputs["dense_ctx"]).T,
        "w0_a": w0[first, other].reshape(128, 4, N),
        "w0_b": w0[other, first].reshape(128, 4, N),
        "w0_a16": w0[half, half + WRAP],
        "w0_b16": w0[half + WRAP, half],
        "w1": w1.reshape(128, GROUPS, SUB * N),
        "w_top1": np.asarray(inputs["W_top1"]),
        "b_top1": columns(inputs["b_top1"], H1 // 128),
        "w_top2": np.asarray(inputs["W_top2"]),
        "b_top2": columns(inputs["b_top2"], H2 // 128),
        "w_top3": columns(inputs["W_top3"], H2 // 128),
    }
    arrays = {name: np.ascontiguousarray(a) for name, a in arrays.items()}
    nc = bacc.Bacc("TRN2", target_bir_lowering=False, num_devices=1)
    args = {name: nc.dram_tensor(name, a.shape, mybir.dt.from_np(a.dtype), kind="ExternalInput").ap()
            for name, a in arrays.items()}
    out = nc.dram_tensor("out", (B, 1), F32, kind="ExternalOutput").ap()
    build_cin_tower(nc, **args, out=out)
    return run_bass_kernel_spmd(nc, [arrays], core_ids=[0]).results[0]["out"]
```

```python
from contextlib import ExitStack

import numpy as np

import concourse.bass as bass
from concourse import mybir

F32 = mybir.dt.float32
F32R = mybir.dt.float32r
I32 = mybir.dt.int32
ALU = mybir.AluOpType
ACT = mybir.ActivationFunctionType
AX = mybir.AxisListType

B, F, D = 512, 32, 32
N = 128
COLS = 512
CB = COLS // D
CHUNKS = B // CB
GATHERS = CB * F // 128
WRAP = F // 2
GROUPS = 8
SUB = 4
RING = 4
KIND = "PPFF PPPF PPPV PPPV PPVV VFFF PPPV PPPF".split()
CUTS = [(k.count("P"), k.count("P") + k.count("V")) for k in KIND]
BY_POOL = [g for g in range(GROUPS) if "P" in KIND[g]]
BY_VEC = [g for g in range(GROUPS) if "V" in KIND[g]]
SPLIT = [g for g in range(GROUPS) if CUTS[g][1]]
WHOLE = [g for g in range(GROUPS) if "F" in KIND[g]]
TILES_SPLIT = [(g, j) for g in range(GROUPS) for j in range(CUTS[g][1])]
TILES_WHOLE = [(g, j) for g in range(GROUPS) for j in range(CUTS[g][1], SUB)]
H1, H2, DENSE = 512, 256, 16
EARLY = (CHUNKS - 2) * CB


def upto(kinds, g):
    return kinds.index(g) + 1


def build_cin_tower(nc, tables, ids, dense_t, w0_a, w0_b, w0_a16, w0_b16, w1, w_top1, b_top1,
                    w_top2, b_top2, w_top3, out):
    ctx = ExitStack()
    with ctx:
        def sb(name, shape, dt=F32):
            return ctx.enter_context(nc.sbuf_tensor(name, shape, dt))

        def ps(name, shape):
            return ctx.enter_context(nc.psum_tensor(name, shape, F32))

        def sem(name):
            return ctx.enter_context(nc.semaphore(name))

        x_dram = nc.dram_tensor("x_dram", [CHUNKS, F + WRAP, COLS], F32, kind="Internal").ap()

        ids_base = sb("ids_base", [128, 2, CHUNKS * GATHERS], I32)
        rows = sb("rows", [128, CHUNKS * GATHERS], I32)
        rows_now = sb("rows_now", [128, 2, GATHERS], I32)
        gathered = sb("gathered", [128, 2, GATHERS, D])
        A = sb("A", [128, GROUPS, COLS])
        R = sb("R", [128, 4, COLS])
        X = sb("X", [128, 2, COLS])
        Bm = sb("Bm", [128, 2, SUB, COLS])
        z1 = sb("z1", [128, 4, COLS])
        z16 = sb("z16", [128, COLS])
        z16_parts = sb("z16_parts", [128, COLS], F32R)
        v = sb("v", [128, COLS])
        z = sb("z", [128, RING, SUB * COLS])
        z_hi = sb("z_hi", [128, RING, SUB * COLS], F32R)
        z_lo = sb("z_lo", [128, RING, SUB * COLS], F32R)
        w0 = sb("w0", [128, 4, N])
        w016 = sb("w016", [128, N])
        w016_parts = sb("w016_parts", [128, N], F32R)
        w1_full = sb("w1_full", [128, len(TILES_WHOLE), N])
        w1_hi = sb("w1_hi", [128, len(TILES_SPLIT), N], F32R)
        w1_lo = sb("w1_lo", [128, len(TILES_SPLIT), N], F32R)
        s1 = sb("s1", [128, B])
        s2 = sb("s2", [128, B])
        dense = sb("dense", [DENSE, B])
        wt1 = sb("wt1", [128, 2, H1])
        wt1_dense = sb("wt1_dense", [DENSE, H1])
        wt2 = sb("wt2", [128, H1 // 128, H2])
        wt3 = sb("wt3", [128, H2 // 128])
        bt1 = sb("bt1", [128, H1 // 128])
        bt2 = sb("bt2", [128, H2 // 128])
        y = sb("y", [1, B])
        w0_other = z[:, RING - 1, 0:4 * N].rearrange("p (t n) -> p t n", n=N)
        w016_other = z[:, RING - 1, 4 * N:5 * N]
        w1_raw = z[:, 0:2, :].rearrange("p r (t n) -> p (r t) n", n=N)
        h1 = R
        h2 = z1[:, 0:H2 // 128, :]

        A_ps = ps("A_ps", [128, 2, COLS])
        X_ps = ps("X_ps", [128, COLS])
        acc1 = ps("acc1", [128, COLS])
        acc2 = ps("acc2", [128, 2, COLS])
        top = ps("top", [128, 2, COLS])

        ids_in = sem("ids_in")
        w0_in = sem("w0_in")
        w1_in = sem("w1_in")
        tower_in = sem("tower_in")
        rows_ready = sem("rows_ready")
        rows_staged = sem("rows_staged")
        gather_done = [sem(f"gather_done{p}") for p in range(2)]
        x_written = sem("x_written")
        r_loaded = sem("r_loaded")
        a_loaded = [sem(f"a_loaded{h}") for h in range(2)]
        b_loaded = sem("b_loaded")
        w0_summed = sem("w0_summed")
        w016_hi_ready = sem("w016_hi_ready")
        w016_lo_ready = sem("w016_lo_ready")
        w1_hi_ready = sem("w1_hi_ready")
        w1_lo_ready = sem("w1_lo_ready")
        x_copied = sem("x_copied")
        a_copied = sem("a_copied")
        z1_ready = sem("z1_ready")
        z16_ready = sem("z16_ready")
        z16_hi_ready = sem("z16_hi_ready")
        z16_lo_ready = sem("z16_lo_ready")
        l1_done = sem("l1_done")
        u_ready = sem("u_ready")
        s1_ready = sem("s1_ready")
        z_ready = sem("z_ready")
        z_hi_ready = sem("z_hi_ready")
        z_lo_pool = sem("z_lo_pool")
        z_lo_vec = sem("z_lo_vec")
        mm_done = sem("mm_done")
        v_ready = sem("v_ready")
        s2_ready = sem("s2_ready")
        top_done = sem("top_done")
        h_ready = sem("h_ready")
        y_ready = sem("y_ready")
        out_written = sem("out_written")

        def wait_count(eng, s, count):
            if not (isinstance(count, int) and count <= 0):
                eng.wait_ge(s, count)

        def steps(eng, step):
            step(0, 0, 0)
            step(1, 0, 1)
            with eng.Fori(1, CHUNKS // 2 - 2) as i:
                for p in range(2):
                    step(2 * i + p, i, p)
            for c in range(CHUNKS - 4, CHUNKS):
                step(c, c // 2, c % 2)

        def exists(c, ahead):
            return not isinstance(c, int) or c + ahead < CHUNKS

        AT_X = {False: 2, True: 5}
        AT_L1 = {False: 1, True: 3}
        AT_U = {False: 5, True: 6}
        AT_S1 = {False: 6, True: 7}
        AT_V = 2
        AT_S2 = 6

        units = [(1, m) for m in range(H1 // 128)] + [(2, m) for m in range(H2 // 128)] + [(3, 0)]
        U = len(units)

        block = ctx.enter_context(nc.Block())

        @block.sync
        def _(sp):
            def write_x(n_half, q):
                sp.wait_ge(gather_done[q], 16 * GATHERS * (n_half + 1))
                n = 2 * n_half + q
                src = gathered[:, q, :, :].rearrange("p j d -> p (j d)")
                sp.dma_start(x_dram[n, 0:F, :].rearrange("f (s c) -> (f s) c", s=4), src)\
                    .then_inc(x_written, 16)
                sp.dma_start(x_dram[n, F:F + WRAP, :].rearrange("f (s c) -> (f s) c", s=4), src[0:4 * WRAP, :])\
                    .then_inc(x_written, 16)

            def load_r(n_half, q):
                n = 2 * n_half + q
                wait_count(sp, z1_ready, n)
                wait_count(sp, x_copied, n)
                sp.wait_ge(x_written, 32 * (n + 1))
                x = x_dram[n, :, :]
                for k in range(4):
                    rot = bass.AP(tensor=x.tensor, offset=x.offset + 4 * k * COLS, ap=[[COLS, F], [1, 4 * COLS]],
                                  runtime_checks=x.runtime_checks)
                    sp.dma_start(R[F * k:F * k + F, :, :].rearrange("p t c -> p (t c)"), rot).then_inc(r_loaded, 16)
                    two = bass.AP(tensor=x.tensor, offset=x.offset, ap=[[COLS, F], [WRAP * COLS, 2], [1, COLS]],
                                  runtime_checks=x.runtime_checks)
                    sp.dma_start(X[F * k:F * k + F, :, :], two).then_inc(r_loaded, 16)

            def load_a(n, half):
                for k in range(4):
                    g0 = half * GROUPS // 2
                    src = x_dram[n, 8 * k + g0:8 * k + g0 + GROUPS // 2, :].rearrange("f c -> (f c)")
                    sp.dma_start(A[32 * k:32 * k + 32, g0:g0 + GROUPS // 2, :].rearrange("p g c -> p (g c)"),
                                 src.partition_broadcast(32)).then_inc(a_loaded[half], 16)

            def load_b(p):
                for j in range(1, SUB):
                    cut = 128 - 32 * j
                    sp.dma_start(Bm[0:cut, p, j, :], Bm[32 * j:128, p, 0, :]).then_inc(b_loaded, 16)
                    sp.dma_start(Bm[cut:128, p, j, :], Bm[0:32 * j, p, 0, :]).then_inc(b_loaded, 16)

            sp.dma_start(ids_base[:, :, :], ids).then_inc(ids_in, 16)
            write_x(0, 0)
            load_r(0, 0)
            load_a(0, 0)
            sp.wait_ge(u_ready, 1)
            load_b(0)
            load_a(0, 1)
            write_x(0, 1)
            load_r(0, 1)
            for dst, src in ((wt1[:, :, :], w_top1[0:2 * N, :].rearrange("(k p) n -> p k n", p=128)),
                             (wt1_dense[:, :], w_top1[2 * N:2 * N + DENSE, :]),
                             (wt2[:, :, :], w_top2.rearrange("(k p) n -> p k n", p=128)),
                             (wt3[:, :], w_top3), (bt1[:, :], b_top1), (bt2[:, :], b_top2), (dense[:, :], dense_t)):
                sp.dma_start(dst, src).then_inc(tower_in, 16)

            def step(c, i, p):
                if exists(c, 2):
                    write_x(i + 1, p)
                    load_r(i + 1, p)
                if exists(c, 1):
                    sp.wait_ge(a_copied, GROUPS * c + GROUPS // 2)
                    load_a(c + 1, 0)
                    sp.wait_ge(u_ready, c + 2)
                    load_b(1 - p)
                    sp.wait_ge(a_copied, GROUPS * c + GROUPS)
                    load_a(c + 1, 1)

            steps(sp, step)
            sp.wait_ge(y_ready, 2)
            sp.dma_start(out.rearrange("b o -> o b"), y[:, :]).then_inc(out_written, 16)
            sp.wait_ge(out_written, 16)

        @block.gpsimd
        def _(pool):
            def stage_rows(n_half, q):
                n = 2 * n_half + q
                wait_count(pool, x_written, 32 * (n - 1))
                pool.tensor_copy(rows_now[:, q, :], rows[:, bass.ds(GATHERS * n, GATHERS)]).then_inc(rows_staged, 1)
                pool.wait_ge(rows_staged, n + 1)

            def gather(q, j):
                pool.indirect_dma_start(gathered[:, q, j, :], None, tables,
                                        bass.IndirectOffsetOnAxis(ap=rows_now[:, q, j:j + 1], axis=0))\
                    .then_inc(gather_done[q], 16)

            pool.wait_ge(ids_in, 16)
            pool.tensor_tensor(rows[:, :], ids_base[:, 0, :], ids_base[:, 1, :], ALU.add).then_inc(rows_ready, 1)
            pool.wait_ge(rows_ready, 1)
            for n_half, q in ((0, 0), (0, 1), (1, 0)):
                stage_rows(n_half, q)
                for j in range(GATHERS):
                    gather(q, j)

            def step(c, i, p):
                n_half, q = i + 1 + p, 1 - p
                if exists(c, 3):
                    stage_rows(n_half, q)
                for n in range(max(GATHERS, len(BY_POOL))):
                    if n < len(BY_POOL):
                        g = BY_POOL[n]
                        pool.wait_ge(z_hi_ready, len(SPLIT) * c + upto(SPLIT, g))
                        wait_count(pool, mm_done, GROUPS * c + g - RING + 1)
                        part = slice(0, COLS * CUTS[g][0])
                        pool.tensor_tensor(z_lo[:, g % RING, part], z[:, g % RING, part],
                                           z_hi[:, g % RING, part].bitcast(F32), ALU.subtract).then_inc(z_lo_pool, 1)
                    if n < GATHERS and exists(c, 3):
                        gather(q, n)

            steps(pool, step)

        @block.scalar
        def _(act):
            def copy_x(c):
                act.wait_ge(r_loaded, 128 * (c + 1))
                wait_count(act, z1_ready, c)
                act.activation(X_ps[:, :], X[:, 0, :], ACT.Copy).then_inc(x_copied, 1)

            def round_z16(c):
                act.wait_ge(z16_ready, c + 1)
                wait_count(act, l1_done, c)
                act.activation(z16_parts[:, :], z16[:, :], ACT.Copy).then_inc(z16_hi_ready, 1)

            def relu_u(c, p):
                act.wait_ge(l1_done, c + 1)
                wait_count(act, z_ready, GROUPS * (c - 1))
                wait_count(act, s1_ready, c - 1)
                act.activation(Bm[:, p, 0, :], acc1[:, :], ACT.Relu).then_inc(u_ready, 1)

            def relu_v(c, p):
                act.wait_ge(mm_done, GROUPS * (c + 1))
                wait_count(act, s2_ready, c)
                act.activation(v[:, :], acc2[:, p, :], ACT.Relu).then_inc(v_ready, 1)

            def copy_a(c, g):
                act.wait_ge(a_loaded[g // (GROUPS // 2)], 64 * (c + 1))
                wait_count(act, z_ready, GROUPS * c + g - 1)
                act.activation(A_ps[:, g % 2, :], A[:, g, :], ACT.Copy).then_inc(a_copied, 1)

            def unit_out(n, b0, b1, count):
                layer, m = units[n]
                act.wait_ge(top_done, count)
                src = top[:, n % 2, 0:b1 - b0]
                if layer == 1:
                    act.activation(h1[:, m, b0:b1], src, ACT.Relu, bias=bt1[:, m:m + 1]).then_inc(h_ready, 1)
                elif layer == 2:
                    act.activation(h2[:, m, b0:b1], src, ACT.Relu, bias=bt2[:, m:m + 1]).then_inc(h_ready, 1)
                else:
                    act.activation(y[:, b0:b1], src[0:1, :], ACT.Copy).then_inc(y_ready, 1)

            act.dma_start(w0[:, :, :], w0_a).then_inc(w0_in, 16)
            act.dma_start(w016[:, :], w0_a16).then_inc(w0_in, 16)
            act.dma_start(w0_other, w0_b).then_inc(w0_in, 16)
            act.dma_start(w016_other, w0_b16).then_inc(w0_in, 16)
            act.dma_start(w1_raw[:, 0:len(TILES_SPLIT), :], w1[:, 0:len(TILES_SPLIT), :]).then_inc(w1_in, 16)
            act.dma_start(w1_full[:, :, :], w1[:, len(TILES_SPLIT):, :]).then_inc(w1_in, 16)
            act.wait_ge(w0_summed, 1)
            act.activation(w016_parts[:, :], w016[:, :], ACT.Copy).then_inc(w016_hi_ready, 1)
            act.wait_ge(w1_in, 32)
            act.activation(w1_hi[:, :, :], w1_raw[:, 0:len(TILES_SPLIT), :], ACT.Copy).then_inc(w1_hi_ready, 1)
            copy_x(0)
            round_z16(0)
            copy_a(0, 0)
            relu_u(0, 0)

            def step(c, i, p):
                first, last = isinstance(c, int) and c == 0, isinstance(c, int) and c == CHUNKS - 1
                for g in range(GROUPS):
                    if g == AT_X[first] - 1 and exists(c, 1):
                        copy_x(c + 1)
                    if g + 1 < GROUPS:
                        copy_a(c, g + 1)
                    elif exists(c, 1):
                        copy_a(c + 1, 0)
                    if g == AT_X[first] and exists(c, 1):
                        round_z16(c + 1)
                    if g in SPLIT:
                        act.wait_ge(z_ready, GROUPS * c + g + 1)
                        wait_count(act, mm_done, GROUPS * c + g - RING + 1)
                        part = slice(0, COLS * CUTS[g][1])
                        act.activation(z_hi[:, g % RING, part], z[:, g % RING, part], ACT.Copy).then_inc(z_hi_ready, 1)
                    if g == AT_V and not first:
                        relu_v(c - 1, 1 - p)
                    if g == AT_U[first] and exists(c, 1):
                        relu_u(c + 1, 1 - p)
                    if last and g == 0:
                        act.wait_ge(tower_in, 16 * 7)
                    if last and 1 <= g <= U:
                        unit_out(g - 1, 0, EARLY, g)
                if last:
                    for n in range(GROUPS - 1, U):
                        unit_out(n, 0, EARLY, n + 1)

            steps(act, step)
            relu_v(CHUNKS - 1, 1)
            for n in range(U):
                unit_out(n, EARLY, B, U + n + 1)

        @block.vector
        def _(dve):
            def layer1_products(c):
                dve.wait_ge(x_copied, c + 1)
                dve.wait_ge(r_loaded, 128 * (c + 1))
                wait_count(dve, z16_lo_ready, c)
                dve.tensor_tensor(z16[:, :], X_ps[:, :], X[:, 1, :], ALU.mult).then_inc(z16_ready, 1)
                wait_count(dve, l1_done, c)
                dve.tensor_tensor(z1[:, :, :], X_ps[:, :].unsqueeze(1).to_broadcast([128, 4, COLS]), R[:, :, :],
                                  ALU.mult).then_inc(z1_ready, 1)
                dve.wait_ge(z16_hi_ready, c + 1)
                dve.tensor_tensor(z16_parts[64:128, :], z16[64:128, :], z16_parts[64:128, :].bitcast(F32),
                                  ALU.subtract).then_inc(z16_lo_ready, 1)

            def sum_u(c, p):
                dve.wait_ge(u_ready, c + 1)
                dve.tensor_reduce(s1[:, bass.ds(CB * c, CB)], Bm[:, p, 0, :].rearrange("p (b d) -> p b d", d=D), AX.X, ALU.add)\
                    .then_inc(s1_ready, 1)

            def sum_v(c):
                dve.wait_ge(v_ready, c + 1)
                dve.tensor_reduce(s2[:, bass.ds(CB * c, CB)], v[:, :].rearrange("p (b d) -> p b d", d=D), AX.X, ALU.add)\
                    .then_inc(s2_ready, 1)

            def wait_slot_free(c, g):
                before, cc = (g - RING, c) if g >= RING else (g - RING + GROUPS, c - 1)
                if before in WHOLE:
                    wait_count(dve, mm_done, GROUPS * cc + before + 1)
                    return
                if before in BY_POOL:
                    wait_count(dve, z_lo_pool, len(BY_POOL) * cc + upto(BY_POOL, before))
                if before in BY_VEC:
                    wait_count(dve, z_lo_vec, len(BY_VEC) * cc + upto(BY_VEC, before))

            def low_part(c, g):
                dve.wait_ge(z_hi_ready, len(SPLIT) * c + upto(SPLIT, g))
                wait_count(dve, mm_done, GROUPS * c + g - RING + 1)
                part = slice(COLS * CUTS[g][0], COLS * CUTS[g][1])
                dve.tensor_tensor(z_lo[:, g % RING, part], z[:, g % RING, part], z_hi[:, g % RING, part].bitcast(F32),
                                  ALU.subtract).then_inc(z_lo_vec, 1)

            dve.wait_ge(w0_in, 64)
            dve.tensor_tensor(w016[:, :], w016[:, :], w016_other, ALU.add).then_inc(w0_summed, 1)
            dve.tensor_tensor(w0[:, 1:4, :], w0[:, 1:4, :], w0_other[:, 1:4, :], ALU.add).then_inc(w0_summed, 1)
            for k in range(1, 4):
                dve.tensor_tensor(w0[F * k:F * k + F, 0, :], w0[F * k:F * k + F, 0, :],
                                  w0_other[F * k:F * k + F, 0, :], ALU.add).then_inc(w0_summed, 1)
            dve.wait_ge(w016_hi_ready, 1)
            for k in (1, 3):
                dve.tensor_tensor(w016_parts[F * k:F * k + F, :], w016[F * k:F * k + F, :],
                                  w016_parts[F * k:F * k + F, :].bitcast(F32), ALU.subtract).then_inc(w016_lo_ready, 1)
            dve.wait_ge(w1_hi_ready, 1)
            dve.tensor_tensor(w1_lo[:, :, :], w1_raw[:, 0:len(TILES_SPLIT), :], w1_hi[:, :, :].bitcast(F32),
                              ALU.subtract).then_inc(w1_lo_ready, 1)
            layer1_products(0)
            dve.wait_ge(w1_lo_ready, 1)
            dve.wait_ge(w0_summed, 5)

            def step(c, i, p):
                first = isinstance(c, int) and c == 0
                for g in range(GROUPS):
                    if g == AT_X[first] and exists(c, 1):
                        layer1_products(c + 1)
                    if g == 0:
                        dve.wait_ge(b_loaded, 96 * (c + 1))
                    dve.wait_ge(a_copied, GROUPS * c + g + 1)
                    wait_slot_free(c, g)
                    dve.tensor_tensor(z[:, g % RING, :].rearrange("p (j c) -> p j c", c=COLS),
                                      A_ps[:, g % 2, :].unsqueeze(1).to_broadcast([128, SUB, COLS]),
                                      Bm[:, p, :, :], ALU.mult).then_inc(z_ready, 1)
                    if g - 1 in BY_VEC:
                        low_part(c, g - 1)
                    if first and g == 0:
                        sum_u(0, 0)
                    if g == AT_S2 and not first:
                        sum_v(c - 1)
                    if g == AT_S1[first] and exists(c, 1):
                        sum_u(c + 1, 1 - p)
                if GROUPS - 1 in BY_VEC:
                    low_part(c, GROUPS - 1)

            steps(dve, step)
            sum_v(CHUNKS - 1)

        @block.tensor
        def _(pe):
            def layer1(c):
                pe.wait_ge(z1_ready, c + 1)
                wait_count(pe, u_ready, c)
                for t in range(4):
                    pe.matmul(acc1[:, :], w0[:, t, :], z1[:, t, :], start=(t == 0), stop=False)
                pe.wait_ge(z16_lo_ready, c + 1)
                pe.matmul(acc1[:, :], w016_parts[:, :], z16_parts[:, :], start=False, stop=True).then_inc(l1_done, 1)

            OPENS = (w1_full, z, CUTS[0][1]) if CUTS[0][1] < SUB else (w1_hi, z_hi, 0)
            CLOSES = (w1_full, z, SUB - 1) if not CUTS[-1][1] else \
                     (w1_hi, z_lo, CUTS[-1][0] - 1 if CUTS[-1][0] else CUTS[-1][1] - 1)

            def group(c, g, p):
                acc = acc2[:, p, :]

                def tile(w, kept, zz, j):
                    return pe.matmul(acc, w[:, kept.index((g, j)), :], zz[:, g % RING, COLS * j:COLS * j + COLS],
                                     start=(g == 0 and (w, zz, j) == OPENS), stop=(g == GROUPS - 1 and (w, zz, j) == CLOSES))

                if g in WHOLE:
                    pe.wait_ge(z_ready, GROUPS * c + g + 1)
                    for j in range(CUTS[g][1], SUB):
                        mm = tile(w1_full, TILES_WHOLE, z, j)
                if g in SPLIT:
                    pe.wait_ge(z_hi_ready, len(SPLIT) * c + upto(SPLIT, g))
                    for j in range(CUTS[g][1]):
                        tile(w1_hi, TILES_SPLIT, z_hi, j)
                        tile(w1_lo, TILES_SPLIT, z_hi, j)
                    if g in BY_VEC:
                        pe.wait_ge(z_lo_vec, len(BY_VEC) * c + upto(BY_VEC, g))
                        for j in range(*CUTS[g]):
                            mm = tile(w1_hi, TILES_SPLIT, z_lo, j)
                    if g in BY_POOL:
                        pe.wait_ge(z_lo_pool, len(BY_POOL) * c + upto(BY_POOL, g))
                        for j in range(CUTS[g][0]):
                            mm = tile(w1_hi, TILES_SPLIT, z_lo, j)
                mm.then_inc(mm_done, 1)

            def unit(n, b0, b1, h_before):
                layer, m = units[n]
                M = 1 if layer == 3 else 128
                dst = top[0:M, n % 2, 0:b1 - b0]
                if layer == 1:
                    wait_count(pe, h_ready, h_before + n - 1)
                    terms = [(wt1[:, 0, 128 * m:128 * m + 128], s1[:, b0:b1]), (wt1[:, 1, 128 * m:128 * m + 128], s2[:, b0:b1]),
                             (wt1_dense[:, 128 * m:128 * m + 128], dense[:, b0:b1])]
                elif layer == 2:
                    pe.wait_ge(h_ready, h_before + (H1 // 128 if m == 0 else n - 1))
                    terms = [(wt2[:, k, 128 * m:128 * m + 128], h1[:, k, b0:b1]) for k in range(H1 // 128)]
                else:
                    pe.wait_ge(h_ready, h_before + n)
                    terms = [(wt3[:, k:k + 1], h2[:, k, b0:b1]) for k in range(H2 // 128)]
                for k, (w, rhs) in enumerate(terms):
                    mm = pe.matmul(dst, w, rhs, start=(k == 0), stop=(k == len(terms) - 1))
                mm.then_inc(top_done, 1)

            pe.wait_ge(w0_summed, 5)
            pe.wait_ge(w016_lo_ready, 2)
            layer1(0)
            pe.wait_ge(w1_in, 32)
            pe.wait_ge(w1_lo_ready, 1)

            def step(c, i, p):
                wait_count(pe, v_ready, c - 1)
                first, last = isinstance(c, int) and c == 0, isinstance(c, int) and c == CHUNKS - 1
                if last:
                    pe.wait_ge(tower_in, 16 * 7)
                    pe.wait_ge(s2_ready, CHUNKS - 2)
                    pe.wait_ge(s1_ready, CHUNKS)
                for g in range(GROUPS):
                    group(c, g, p)
                    if g == AT_L1[first] and exists(c, 1):
                        layer1(c + 1)
                    if last and g < U:
                        unit(g, 0, EARLY, 0)

            steps(pe, step)
            pe.wait_ge(s2_ready, CHUNKS)
            pe.wait_ge(y_ready, 1)
            for n in range(U):
                unit(n, EARLY, B, U - 1)


_TABLES = [f"tbl_{f}" for f in range(F)]


def kernel(**inputs):
    import concourse.bacc as bacc
    from concourse.bass_utils import run_bass_kernel_spmd

    tables = np.concatenate([np.asarray(inputs[t]) for t in _TABLES], axis=0)
    sizes = [np.asarray(inputs[t]).shape[0] for t in _TABLES]
    starts = np.array([sum(sizes[:f]) for f in range(F)], np.int32)
    ids = np.asarray(inputs["ids"]).T.reshape(F, CHUNKS, 4, GATHERS).transpose(0, 2, 1, 3).reshape(128, -1)
    row_base = np.broadcast_to(starts[:, None, None], (F, 4, CHUNKS * GATHERS)).reshape(128, -1).astype(ids.dtype)
    w0 = np.asarray(inputs["L0_rec_filter_0"])[0].reshape(F, F, N)
    h = np.arange(F)
    first = np.tile(h[None, :, None], (4, 1, 4))
    other = (first + 4 * np.arange(4)[:, None, None] + np.arange(4)) % F
    half = np.arange(WRAP)
    pad = lambda a: np.tile(np.concatenate([a, np.zeros_like(a)]), (4, 1))
    w1 = np.asarray(inputs["L0_rec_filter_1"])[0].reshape(4, GROUPS, 4, 32, N)
    q, r, g, j = np.ogrid[0:4, 0:32, 0:GROUPS, 0:SUB]
    w1 = w1[q, g, (q + j) % 4, r].reshape(128, GROUPS * SUB, N)[:, [SUB * g + j for g, j in TILES_SPLIT + TILES_WHOLE]]
    columns = lambda a, n: np.asarray(a).reshape(n, 128).T
    arrays = {
        "tables": tables,
        "ids": np.stack([ids, row_base], axis=1),
        "dense_t": np.asarray(inputs["dense_ctx"]).T,
        "w0_a": w0[first, other].reshape(128, 4, N),
        "w0_b": w0[other, first].reshape(128, 4, N),
        "w0_a16": pad(w0[half, half + WRAP]),
        "w0_b16": pad(w0[half + WRAP, half]),
        "w1": w1,
        "w_top1": np.asarray(inputs["W_top1"]),
        "b_top1": columns(inputs["b_top1"], H1 // 128),
        "w_top2": np.asarray(inputs["W_top2"]),
        "b_top2": columns(inputs["b_top2"], H2 // 128),
        "w_top3": columns(inputs["W_top3"], H2 // 128),
    }
    arrays = {name: np.ascontiguousarray(a) for name, a in arrays.items()}
    nc = bacc.Bacc("TRN2", target_bir_lowering=False, num_devices=1)
    args = {name: nc.dram_tensor(name, a.shape, mybir.dt.from_np(a.dtype), kind="ExternalInput").ap()
            for name, a in arrays.items()}
    out = nc.dram_tensor("out", (B, 1), F32, kind="ExternalOutput").ap()
    build_cin_tower(nc, **args, out=out)
    return run_bass_kernel_spmd(nc, [arrays], core_ids=[0]).results[0]["out"]
```

```python
from contextlib import ExitStack

import numpy as np

import concourse.bass as bass
from concourse import mybir

F32 = mybir.dt.float32
F32R = mybir.dt.float32r
I32 = mybir.dt.int32
ALU = mybir.AluOpType
ACT = mybir.ActivationFunctionType
AX = mybir.AxisListType

B, F, D = 512, 32, 32
N = 128
COLS = 512
CB = COLS // D
CHUNKS = B // CB
GATHERS = CB * F // 128
WRAP = F // 2
GROUPS = 8
SUB = 4
RING = 4
A_BANKS = 4
A_AHEAD = 1
KIND = "PPFF PPPF PVVF PPFF PPVV PPVF PPPV PPPF".split()
KIND_LAST = "PPFF PPPF PVVF PPFF PPVV PPVF PVVV PVVF".split()


def cuts(kind):
    return [(k.count("P"), k.count("P") + k.count("V")) for k in kind]


CUTS, CUTS_LAST = cuts(KIND), cuts(KIND_LAST)
SPLIT = [g for g in range(GROUPS) if CUTS[g][1]]
WHOLE = [g for g in range(GROUPS) if "F" in KIND[g]]
TILES_SPLIT = [(g, j) for g in range(GROUPS) for j in range(CUTS[g][1])]
TILES_WHOLE = [(g, j) for g in range(GROUPS) for j in range(CUTS[g][1], SUB)]
RAW_TILES = 8
RAW_PARTS = -(-len(TILES_SPLIT) // RAW_TILES)
H1, H2 = 512, 256
WARM_UP = 16
EARLY = (CHUNKS - 2) * CB


def is_last(c):
    return isinstance(c, int) and c == CHUNKS - 1


def cuts_of(c):
    return CUTS_LAST if is_last(c) else CUTS


def by_pool(c):
    return [g for g in range(GROUPS) if cuts_of(c)[g][0]]


def by_vec(c):
    return [g for g in range(GROUPS) if cuts_of(c)[g][1] > cuts_of(c)[g][0]]


def hi_count(c, g):
    return len(SPLIT) * c + SPLIT.index(g) + 1


def pool_count(c, g):
    return len(by_pool(0)) * c + by_pool(c).index(g) + 1


def vec_count(c, g):
    return len(by_vec(0)) * c + by_vec(c).index(g) + 1


def build_cin_tower(nc, tables, ids, dense_t, w0_a, w0_b, w0_a16, w0_b16, w1, w_top1, w_top1_dense, b_top1,
                    w_top2, b_top2, w_top3, out):
    ctx = ExitStack()
    with ctx:
        def sb(name, shape, dt=F32):
            return ctx.enter_context(nc.sbuf_tensor(name, shape, dt))

        def ps(name, shape):
            return ctx.enter_context(nc.psum_tensor(name, shape, F32))

        def sem(name):
            return ctx.enter_context(nc.semaphore(name))

        x_dram = nc.dram_tensor("x_dram", [CHUNKS, F + WRAP, COLS], F32, kind="Internal").ap()

        ids_base = sb("ids_base", [128, 2, CHUNKS * GATHERS], I32)
        rows = sb("rows", [128, CHUNKS * GATHERS], I32)
        rows_now = sb("rows_now", [128, 2, GATHERS], I32)
        gathered = sb("gathered", [128, 2, GATHERS, D])
        A = sb("A", [128, GROUPS, COLS])
        R = sb("R", [128, 4, COLS])
        X = sb("X", [128, 2, COLS])
        Bm = sb("Bm", [128, 2, SUB, COLS])
        z1 = sb("z1", [128, 4, COLS])
        z16 = sb("z16", [128, COLS])
        z16_parts = sb("z16_parts", [128, COLS], F32R)
        v = sb("v", [128, COLS])
        z = sb("z", [128, RING, SUB * COLS])
        z_hi = sb("z_hi", [128, RING, SUB * COLS], F32R)
        z_lo = sb("z_lo", [128, RING, SUB * COLS], F32R)
        w0 = sb("w0", [128, 4, N])
        w016 = sb("w016", [128, N])
        w016_parts = sb("w016_parts", [128, N], F32R)
        w1_full = sb("w1_full", [128, len(TILES_WHOLE), N])
        w1_hi = sb("w1_hi", [128, len(TILES_SPLIT), N], F32R)
        w1_lo = sb("w1_lo", [128, len(TILES_SPLIT), N], F32R)
        s1 = sb("s1", [128, B])
        s2 = sb("s2", [128, B])
        wt1 = sb("wt1", [128, 2, H1])
        wt1_dense_parts = sb("wt1_dense_parts", [128, H1], F32R)
        wt2 = sb("wt2", [128, H1 // 128, H2])
        wt3 = sb("wt3", [128, H2 // 128])
        bt1 = sb("bt1", [128, H1 // 128])
        bt2 = sb("bt2", [128, H2 // 128])
        y = sb("y", [1, B])
        w0_other = z[:, 0, 0:4 * N].rearrange("p (t n) -> p t n", n=N)
        w016_other = z[:, 0, 4 * N:5 * N]
        w1_raw = z[:, RING - 2:RING, :].rearrange("p r (t n) -> p (r t) n", n=N)
        dense, wt1_dense = X[:, 0, 0:B], X[:, 1, 0:H1]
        dense_parts = z16_parts[:, 0:B]
        h1 = R
        h2 = z1[:, 0:H2 // 128, :]

        A_ps = ps("A_ps", [128, A_BANKS, COLS])
        acc2 = ps("acc2", [128, 2, COLS])
        top = ps("top", [128, 2, COLS])
        X_ps, acc1 = top[:, 0, :], top[:, 1, :]

        ids_in = sem("ids_in")
        w0_in = sem("w0_in")
        w1_full_in = sem("w1_full_in")
        w1_raw_in = sem("w1_raw_in")
        tower_in = sem("tower_in")
        rows_ready = sem("rows_ready")
        rows_staged = sem("rows_staged")
        gather_done = [sem(f"gather_done{p}") for p in range(2)]
        x_written = sem("x_written")
        x_loaded = sem("x_loaded")
        r_loaded = sem("r_loaded")
        r_first = [sem(f"r_first{half}") for half in range(2)]
        a_loaded = [sem(f"a_loaded{h}") for h in range(2)]
        b_loaded = sem("b_loaded")
        w0_summed = sem("w0_summed")
        w016_hi_ready = sem("w016_hi_ready")
        w016_lo_ready = sem("w016_lo_ready")
        w1_hi_ready = sem("w1_hi_ready")
        w1_lo_ready = sem("w1_lo_ready")
        x_copied = sem("x_copied")
        a_copied = sem("a_copied")
        z1_first = sem("z1_first")
        z1_ready = sem("z1_ready")
        z16_ready = sem("z16_ready")
        z16_hi_ready = sem("z16_hi_ready")
        z16_lo_ready = sem("z16_lo_ready")
        l1_done = sem("l1_done")
        u_ready = sem("u_ready")
        s1_ready = sem("s1_ready")
        b_copied = sem("b_copied")
        z_ready = sem("z_ready")
        z_hi_ready = sem("z_hi_ready")
        z_lo_pool = sem("z_lo_pool")
        z_lo_vec = sem("z_lo_vec")
        mm_done = sem("mm_done")
        v_ready = sem("v_ready")
        s2_ready = sem("s2_ready")
        top_done = sem("top_done")
        dense_in = sem("dense_in")
        dense_hi_ready = sem("dense_hi_ready")
        dense_lo_ready = sem("dense_lo_ready")
        h_ready = sem("h_ready")
        tail_done = sem("tail_done")
        tail_act = sem("tail_act")
        tail_vec = sem("tail_vec")
        y_ready = sem("y_ready")
        out_written = sem("out_written")

        def wait_count(eng, s, count):
            if not (isinstance(count, int) and count <= 0):
                eng.wait_ge(s, count)

        def steps(eng, step):
            step(0, 0, 0)
            step(1, 0, 1)
            with eng.Fori(1, CHUNKS // 2 - 2) as i:
                for p in range(2):
                    step(2 * i + p, i, p)
            for c in range(CHUNKS - 4, CHUNKS):
                step(c, c // 2, c % 2)

        TURNS = [(2, 0, 64, 64), (2, 64, 0, 64)]
        TURNS += [(j, 32 * q, 32 * ((q + j) % 4), 32) for j in (1, 3) for q in range(4)]
        BY_ACT = 4

        def exists(c, ahead):
            return not isinstance(c, int) or c + ahead < CHUNKS

        AT_X = {False: 2, True: 4}
        AT_L1 = {False: 0, True: 2}
        AT_U = {False: 3, True: 4}
        AT_S1 = {False: 6, True: 7}
        AT_V = 2
        AT_S2 = 7

        units = [(1, m) for m in range(H1 // 128)] + [(2, m) for m in range(H2 // 128)] + [(3, 0)]
        U = len(units)
        TAIL1 = [bank[:, 0:B - EARLY] for bank in (top[:, 0, :], top[:, 1, :], A_ps[:, 2, :], A_ps[:, 3, :])]
        TAIL2 = [A_ps[:, 0, 0:B - EARLY], A_ps[:, 1, 0:B - EARLY]]
        TAIL3 = acc2[0:1, 0, 0:B - EARLY]

        block = ctx.enter_context(nc.Block())

        @block.sync
        def _(sp):
            def write_x(n_half, q):
                sp.wait_ge(gather_done[q], 16 * GATHERS * (n_half + 1))
                n = 2 * n_half + q
                src = gathered[:, q, :, :].rearrange("p j d -> p (j d)")
                sp.dma_start(x_dram[n, 0:F, :].rearrange("f (s c) -> (f s) c", s=4), src)\
                    .then_inc(x_written, 16)
                sp.dma_start(x_dram[n, F:F + WRAP, :].rearrange("f (s c) -> (f s) c", s=4), src[0:4 * WRAP, :])\
                    .then_inc(x_written, 16)

            def load_r(n_half, q):
                n = 2 * n_half + q
                wait_count(sp, z1_ready, n)
                wait_count(sp, x_copied, n)
                sp.wait_ge(x_written, 32 * (n + 1))
                x = x_dram[n, :, :]
                for k in range(4):
                    two = bass.AP(tensor=x.tensor, offset=x.offset, ap=[[COLS, F], [WRAP * COLS, 2], [1, COLS]],
                                  runtime_checks=x.runtime_checks)
                    sp.dma_start(X[F * k:F * k + F, :, :], two).then_inc(x_loaded, 16)
                halves = [slice(0, 2), slice(2, 4)] if isinstance(n, int) and n == 0 else [slice(0, 4)]
                for half, tiles in enumerate(halves):
                    for k in range(4):
                        rot = bass.AP(tensor=x.tensor, offset=x.offset + (4 * k + tiles.start) * COLS,
                                      ap=[[COLS, F], [1, (tiles.stop - tiles.start) * COLS]],
                                      runtime_checks=x.runtime_checks)
                        sp.dma_start(R[F * k:F * k + F, tiles, :].rearrange("p t c -> p (t c)"), rot)\
                            .then_inc(r_first[half] if len(halves) == 2 else r_loaded, 16)

            def load_a(n, half):
                for k in range(4):
                    g0 = half * GROUPS // 2
                    src = x_dram[n, 8 * k + g0:8 * k + g0 + GROUPS // 2, :].rearrange("f c -> (f c)")
                    sp.dma_start(A[32 * k:32 * k + 32, g0:g0 + GROUPS // 2, :].rearrange("p g c -> p (g c)"),
                                 src.partition_broadcast(32)).then_inc(a_loaded[half], 16)

            def load_b(p):
                for j in range(1, SUB):
                    cut = 128 - 32 * j
                    sp.dma_start(Bm[0:cut, p, j, :], Bm[32 * j:128, p, 0, :]).then_inc(b_loaded, 16)
                    sp.dma_start(Bm[cut:128, p, j, :], Bm[0:32 * j, p, 0, :]).then_inc(b_loaded, 16)

            sp.dma_start(ids_base[:, :, :], ids).then_inc(ids_in, 16)
            write_x(0, 0)
            load_r(0, 0)
            load_a(0, 0)
            sp.dma_start(w1_full[:, :, :], w1[:, len(TILES_SPLIT):, :]).then_inc(w1_full_in, 16)
            load_a(0, 1)
            write_x(0, 1)
            load_r(0, 1)
            for dst, src in ((wt1[:, :, :], w_top1.rearrange("(k p) n -> p k n", p=128)),
                             (wt2[:, :, :], w_top2.rearrange("(k p) n -> p k n", p=128)),
                             (wt3[:, :], w_top3), (bt1[:, :], b_top1), (bt2[:, :], b_top2)):
                sp.dma_start(dst, src).then_inc(tower_in, 16)

            def step(c, i, p):
                if exists(c, 2):
                    write_x(i + 1, p)
                    load_r(i + 1, p)
                if exists(c, 1):
                    sp.wait_ge(a_copied, GROUPS * c + GROUPS // 2)
                    load_a(c + 1, 0)
                    sp.wait_ge(u_ready, c + 2)
                    if isinstance(c, int) and c == CHUNKS - 2:
                        sp.dma_start(dense, dense_t).then_inc(dense_in, 16)
                        sp.dma_start(wt1_dense, w_top1_dense).then_inc(dense_in, 16)
                    load_b(1 - p)
                    sp.wait_ge(a_copied, GROUPS * c + GROUPS)
                    load_a(c + 1, 1)

            steps(sp, step)
            sp.wait_ge(y_ready, 2)
            sp.dma_start(out.rearrange("b o -> o b"), y[:, :]).then_inc(out_written, 16)
            sp.wait_ge(out_written, 16)

        @block.gpsimd
        def _(pool):
            def stage_rows(n_half, q):
                n = 2 * n_half + q
                wait_count(pool, x_written, 32 * (n - 1))
                pool.tensor_copy(rows_now[:, q, :], rows[:, bass.ds(GATHERS * n, GATHERS)]).then_inc(rows_staged, 1)
                pool.wait_ge(rows_staged, n + 1)

            def gather(q, j):
                pool.indirect_dma_start(gathered[:, q, j, :], None, tables,
                                        bass.IndirectOffsetOnAxis(ap=rows_now[:, q, j:j + 1], axis=0))\
                    .then_inc(gather_done[q], 16)

            pool.wait_ge(ids_in, 16)
            pool.tensor_tensor(rows[:, :], ids_base[:, 0, :], ids_base[:, 1, :], ALU.add).then_inc(rows_ready, 1)
            pool.wait_ge(rows_ready, 1)
            for n_half, q in ((0, 0), (0, 1), (1, 0)):
                stage_rows(n_half, q)
                for j in range(GATHERS):
                    gather(q, j)
            pool.wait_ge(w1_hi_ready, 1)
            pool.tensor_tensor(w1_lo[:, :, :], w1_raw[:, 0:len(TILES_SPLIT), :], w1_hi[:, :, :].bitcast(F32),
                               ALU.subtract).then_inc(w1_lo_ready, 1)

            def step(c, i, p):
                n_half, q = i + 1 + p, 1 - p
                if exists(c, 3):
                    stage_rows(n_half, q)
                groups = by_pool(c)
                for n in range(max(GATHERS, len(groups))):
                    if n < len(groups):
                        g = groups[n]
                        pool.wait_ge(z_hi_ready, hi_count(c, g))
                        wait_count(pool, mm_done, GROUPS * c + g - RING + 1)
                        part = slice(0, COLS * cuts_of(c)[g][0])
                        pool.tensor_tensor(z_lo[:, g % RING, part], z[:, g % RING, part],
                                           z_hi[:, g % RING, part].bitcast(F32), ALU.subtract).then_inc(z_lo_pool, 1)
                    if n < GATHERS and exists(c, 3):
                        gather(q, n)

            steps(pool, step)

        @block.scalar
        def _(act):
            def copy_x(c):
                act.wait_ge(x_loaded, 64 * (c + 1))
                wait_count(act, z1_ready, c)
                act.activation(X_ps, X[:, 0, :], ACT.Copy).then_inc(x_copied, 1)

            def round_z16(c):
                act.wait_ge(z16_ready, c + 1)
                wait_count(act, l1_done, c)
                act.activation(z16_parts[:, :], z16[:, :], ACT.Copy).then_inc(z16_hi_ready, 1)

            def relu_u(c, p):
                act.wait_ge(l1_done, c + 1)
                wait_count(act, z_ready, GROUPS * (c - 1))
                wait_count(act, s1_ready, c - 1)
                act.activation(Bm[:, p, 0, :], acc1, ACT.Relu).then_inc(u_ready, 1)

            def relu_v(c, p):
                act.wait_ge(mm_done, GROUPS * (c + 1))
                wait_count(act, s2_ready, c)
                act.activation(v[:, :], acc2[:, p, :], ACT.Relu).then_inc(v_ready, 1)

            def copy_a(c, g):
                act.wait_ge(a_loaded[g // (GROUPS // 2)], 64 * (c + 1))
                wait_count(act, z_ready, GROUPS * c + g - A_BANKS + 1)
                act.activation(A_ps[:, g % A_BANKS, :], A[:, g, :], ACT.Copy).then_inc(a_copied, 1)

            def unit_out(n):
                layer, m = units[n]
                act.wait_ge(top_done, n + 1)
                src = top[:, n % 2, 0:EARLY]
                if layer == 1:
                    act.activation(h1[:, m, 0:EARLY], src, ACT.Relu, bias=bt1[:, m:m + 1]).then_inc(h_ready, 1)
                elif layer == 2:
                    act.activation(h2[:, m, 0:EARLY], src, ACT.Relu, bias=bt2[:, m:m + 1]).then_inc(h_ready, 1)
                else:
                    act.activation(y[:, 0:EARLY], src[0:1, :], ACT.Copy).then_inc(y_ready, 1)

            for t in range(0, len(TILES_SPLIT), RAW_TILES):
                end = min(t + RAW_TILES, len(TILES_SPLIT))
                act.dma_start(w1_raw[:, t:end, :], w1[:, t:end, :]).then_inc(w1_raw_in, 16)
            act.dma_start(w016[:, :], w0_a16).then_inc(w0_in, 16)
            act.dma_start(w016_other, w0_b16).then_inc(w0_in, 16)
            act.dma_start(w0[:, :, :], w0_a).then_inc(w0_in, 16)
            act.dma_start(w0_other, w0_b).then_inc(w0_in, 16)
            act.wait_ge(w0_summed, 1)
            act.activation(w016_parts[:, :], w016[:, :], ACT.Copy).then_inc(w016_hi_ready, 1)
            act.wait_ge(w1_raw_in, 16 * RAW_PARTS)
            act.activation(w1_hi[:, :, :], w1_raw[:, 0:len(TILES_SPLIT), :], ACT.Copy).then_inc(w1_hi_ready, 1)
            copy_x(0)
            round_z16(0)
            relu_u(0, 0)
            for j, to, at, size in TURNS[-BY_ACT:]:
                act.activation(Bm[to:to + size, 0, j, :], acc1[at:at + size, :], ACT.Relu).then_inc(b_copied, 1)
            for g in range(A_AHEAD):
                copy_a(0, g)

            def step(c, i, p):
                first, last = isinstance(c, int) and c == 0, isinstance(c, int) and c == CHUNKS - 1
                for g in range(GROUPS):
                    if g == AT_X[first] - 1 and exists(c, 1):
                        copy_x(c + 1)
                    if g + A_AHEAD < GROUPS:
                        copy_a(c, g + A_AHEAD)
                    elif exists(c, 1):
                        copy_a(c + 1, g + A_AHEAD - GROUPS)
                    if g == AT_X[first] and exists(c, 1):
                        round_z16(c + 1)
                    if g in SPLIT:
                        act.wait_ge(z_ready, GROUPS * c + g + 1)
                        wait_count(act, mm_done, GROUPS * c + g - RING + 1)
                        part = slice(0, COLS * CUTS[g][1])
                        act.activation(z_hi[:, g % RING, part], z[:, g % RING, part], ACT.Copy).then_inc(z_hi_ready, 1)
                    if g == AT_V and not first:
                        relu_v(c - 1, 1 - p)
                    if g == AT_U[first] and exists(c, 1):
                        relu_u(c + 1, 1 - p)
                    if isinstance(c, int) and c == CHUNKS - 2 and g == GROUPS - 1:
                        act.wait_ge(dense_in, 32)
                        act.activation(dense_parts, dense, ACT.Copy).then_inc(dense_hi_ready, 1)
                        act.activation(wt1_dense_parts[:, :], wt1_dense, ACT.Copy).then_inc(dense_hi_ready, 1)
                        act.wait_ge(tower_in, 16 * 5)
                    if last and 1 <= g <= U:
                        unit_out(g - 1)
                if last:
                    for n in range(GROUPS - 1, U):
                        unit_out(n)

            steps(act, step)
            relu_v(CHUNKS - 1, 1)
            for m in range(0, H1 // 128, 2):
                act.wait_ge(tail_done, m + 1)
                act.activation(h1[:, m, EARLY:B], TAIL1[m], ACT.Relu, bias=bt1[:, m:m + 1]).then_inc(tail_act, 1)
            act.wait_ge(tail_done, H1 // 128 + 1)
            act.activation(h2[:, 0, EARLY:B], TAIL2[0], ACT.Relu, bias=bt2[:, 0:1]).then_inc(tail_act, 1)

        @block.vector
        def _(dve):
            def layer1_products(c):
                dve.wait_ge(x_copied, c + 1)
                dve.wait_ge(x_loaded, 64 * (c + 1))
                wait_count(dve, z16_lo_ready, c)
                dve.tensor_tensor(z16[:, :], X_ps, X[:, 1, :], ALU.mult).then_inc(z16_ready, 1)
                if isinstance(c, int) and c == 0:
                    for t in range(4):
                        if t % 2 == 0:
                            dve.wait_ge(r_first[t // 2], 64)
                        dve.tensor_tensor(z1[:, t, :], X_ps, R[:, t, :], ALU.mult)\
                            .then_inc(z1_ready if t == 3 else z1_first, 1)
                else:
                    dve.wait_ge(r_loaded, 64 * c)
                    dve.wait_ge(l1_done, c)
                    dve.tensor_tensor(z1[:, :, :], X_ps.unsqueeze(1).to_broadcast([128, 4, COLS]), R[:, :, :],
                                      ALU.mult).then_inc(z1_ready, 1)
                dve.wait_ge(z16_hi_ready, c + 1)
                dve.tensor_tensor(z16_parts[64:128, :], z16[64:128, :], z16_parts[64:128, :].bitcast(F32),
                                  ALU.subtract).then_inc(z16_lo_ready, 1)

            def sum_u(c, p):
                dve.wait_ge(u_ready, c + 1)
                dve.tensor_reduce(s1[:, bass.ds(CB * c, CB)], Bm[:, p, 0, :].rearrange("p (b d) -> p b d", d=D), AX.X, ALU.add)\
                    .then_inc(s1_ready, 1)

            def sum_v(c):
                dve.wait_ge(v_ready, c + 1)
                dve.tensor_reduce(s2[:, bass.ds(CB * c, CB)], v[:, :].rearrange("p (b d) -> p b d", d=D), AX.X, ALU.add)\
                    .then_inc(s2_ready, 1)

            def wait_slot_free(c, g):
                before, cc = (g - RING, c) if g >= RING else (g - RING + GROUPS, c - 1)
                if before in WHOLE:
                    wait_count(dve, mm_done, GROUPS * cc + before + 1)
                    return
                if before in by_pool(cc):
                    wait_count(dve, z_lo_pool, pool_count(cc, before))
                if before in by_vec(cc):
                    wait_count(dve, z_lo_vec, vec_count(cc, before))

            def low_part(c, g):
                dve.wait_ge(z_hi_ready, hi_count(c, g))
                wait_count(dve, mm_done, GROUPS * c + g - RING + 1)
                part = slice(COLS * cuts_of(c)[g][0], COLS * cuts_of(c)[g][1])
                dve.tensor_tensor(z_lo[:, g % RING, part], z[:, g % RING, part], z_hi[:, g % RING, part].bitcast(F32),
                                  ALU.subtract).then_inc(z_lo_vec, 1)

            dve.wait_ge(w0_in, 64)
            dve.tensor_tensor(w016[:, :], w016[:, :], w016_other, ALU.add).then_inc(w0_summed, 1)
            dve.tensor_tensor(w0[:, 1:4, :], w0[:, 1:4, :], w0_other[:, 1:4, :], ALU.add).then_inc(w0_summed, 1)
            for k in range(1, 4):
                dve.tensor_tensor(w0[F * k:F * k + F, 0, :], w0[F * k:F * k + F, 0, :],
                                  w0_other[F * k:F * k + F, 0, :], ALU.add).then_inc(w0_summed, 1)
            dve.wait_ge(w016_hi_ready, 1)
            for k in (1, 3):
                dve.tensor_tensor(w016_parts[F * k:F * k + F, :], w016[F * k:F * k + F, :],
                                  w016_parts[F * k:F * k + F, :].bitcast(F32), ALU.subtract).then_inc(w016_lo_ready, 1)
            layer1_products(0)
            dve.wait_ge(u_ready, 1)
            for j, to, at, size in TURNS[:-BY_ACT]:
                dve.tensor_copy(Bm[to:to + size, 0, j, :], Bm[at:at + size, 0, 0, :]).then_inc(b_copied, 1)
            dve.wait_ge(w0_summed, 5)

            def step(c, i, p):
                first = isinstance(c, int) and c == 0
                for g in range(GROUPS):
                    if g == AT_X[first] and exists(c, 1):
                        layer1_products(c + 1)
                    if g == 0:
                        wait_count(dve, b_loaded, 96 * c)
                        if first:
                            dve.wait_ge(b_copied, len(TURNS))
                    dve.wait_ge(a_copied, GROUPS * c + g + 1)
                    wait_slot_free(c, g)
                    dve.tensor_tensor(z[:, g % RING, :].rearrange("p (j c) -> p j c", c=COLS),
                                      A_ps[:, g % A_BANKS, :].unsqueeze(1).to_broadcast([128, SUB, COLS]),
                                      Bm[:, p, :, :], ALU.mult).then_inc(z_ready, 1)
                    if g - 1 in by_vec(c):
                        low_part(c, g - 1)
                    if first and g == 0:
                        sum_u(0, 0)
                    if first and g == 1:
                        dve.wait_ge(w1_lo_ready, 1)
                    if isinstance(c, int) and c == CHUNKS - 1 and g == 0:
                        dve.wait_ge(dense_hi_ready, 2)
                        dve.tensor_tensor(dense_parts[64:128, :], dense[64:128, :], dense_parts[64:128, :].bitcast(F32),
                                          ALU.subtract).then_inc(dense_lo_ready, 1)
                        for k in (1, 3):
                            dve.tensor_tensor(wt1_dense_parts[F * k:F * k + F, :], wt1_dense[F * k:F * k + F, :],
                                              wt1_dense_parts[F * k:F * k + F, :].bitcast(F32), ALU.subtract)\
                                .then_inc(dense_lo_ready, 1)
                    if g == AT_S2 and not first:
                        sum_v(c - 1)
                    if g == AT_S1[first] and exists(c, 1):
                        sum_u(c + 1, 1 - p)
                if GROUPS - 1 in by_vec(c):
                    low_part(c, GROUPS - 1)

            steps(dve, step)
            sum_v(CHUNKS - 1)
            for m in range(1, H1 // 128, 2):
                dve.wait_ge(tail_done, m + 1)
                dve.tensor_scalar(h1[:, m, EARLY:B], TAIL1[m], bt1[:, m:m + 1], 0.0, ALU.add, ALU.max).then_inc(tail_vec, 1)
            dve.wait_ge(tail_done, H1 // 128 + 2)
            dve.tensor_scalar(h2[:, 1, EARLY:B], TAIL2[1], bt2[:, 1:2], 0.0, ALU.add, ALU.max).then_inc(tail_vec, 1)
            dve.wait_ge(tail_done, H1 // 128 + 3)
            dve.tensor_copy(y[:, EARLY:B], TAIL3).then_inc(y_ready, 1)

        @block.tensor
        def _(pe):
            def layer1(c):
                first = isinstance(c, int) and c == 0
                if not first:
                    pe.wait_ge(z1_ready, c + 1)
                    pe.wait_ge(u_ready, c)
                if isinstance(c, int) and c == 1:
                    pe.wait_ge(b_copied, len(TURNS))
                for t in range(4):
                    if first:
                        pe.wait_ge(*((z1_first, t + 1) if t < 3 else (z1_ready, 1)))
                    pe.matmul(acc1, w0[:, t, :], z1[:, t, :], start=(t == 0), stop=False)
                pe.wait_ge(z16_lo_ready, c + 1)
                pe.matmul(acc1, w016_parts[:, :], z16_parts[:, :], start=False, stop=True).then_inc(l1_done, 1)

            OPENS = (w1_full, z, CUTS[0][1]) if CUTS[0][1] < SUB else (w1_hi, z_hi, 0)

            def group(c, g, p):
                pool_end, vec_end = cuts_of(c)[g]
                closes = (w1_hi, z_lo, (pool_end or vec_end) - 1) if vec_end else (w1_full, z, SUB - 1)

                def tile(w, kept, zz, j):
                    return pe.matmul(acc2[:, p, :], w[:, kept.index((g, j)), :],
                                     zz[:, g % RING, COLS * j:COLS * j + COLS],
                                     start=(g == 0 and (w, zz, j) == OPENS),
                                     stop=(g == GROUPS - 1 and (w, zz, j) == closes))

                if g in WHOLE:
                    pe.wait_ge(z_ready, GROUPS * c + g + 1)
                    for j in range(vec_end, SUB):
                        mm = tile(w1_full, TILES_WHOLE, z, j)
                if g in SPLIT:
                    pe.wait_ge(z_hi_ready, hi_count(c, g))
                    if isinstance(c, int) and c == 0 and g == SPLIT[0]:
                        pe.wait_ge(w1_lo_ready, 1)
                    for j in range(vec_end):
                        tile(w1_hi, TILES_SPLIT, z_hi, j)
                        tile(w1_lo, TILES_SPLIT, z_hi, j)
                    if g in by_vec(c):
                        pe.wait_ge(z_lo_vec, vec_count(c, g))
                        for j in range(pool_end, vec_end):
                            mm = tile(w1_hi, TILES_SPLIT, z_lo, j)
                    if g in by_pool(c):
                        pe.wait_ge(z_lo_pool, pool_count(c, g))
                        for j in range(pool_end):
                            mm = tile(w1_hi, TILES_SPLIT, z_lo, j)
                mm.then_inc(mm_done, 1)

            def unit(n):
                layer, m = units[n]
                block = slice(128 * m, 128 * m + 128)
                dst = top[0:1 if layer == 3 else 128, n % 2, 0:EARLY]
                if layer == 1:
                    wait_count(pe, h_ready, n - 1)
                    terms = [(wt1[:, 0, block], s1[:, 0:EARLY]), (wt1[:, 1, block], s2[:, 0:EARLY]),
                             (wt1_dense_parts[:, block], dense_parts[:, 0:EARLY])]
                elif layer == 2:
                    pe.wait_ge(h_ready, H1 // 128 if m == 0 else n - 1)
                    terms = [(wt2[:, k, block], h1[:, k, 0:EARLY]) for k in range(H1 // 128)]
                else:
                    pe.wait_ge(h_ready, n)
                    terms = [(wt3[:, k:k + 1], h2[:, k, 0:EARLY]) for k in range(H2 // 128)]
                for k, (w, rhs) in enumerate(terms):
                    if n == 0 and k == 2:
                        pe.wait_ge(dense_lo_ready, 3)
                    mm = pe.matmul(dst, w, rhs, start=(k == 0), stop=(k == len(terms) - 1))
                mm.then_inc(top_done, 1)

            def tail():
                rows = slice(EARLY, B)
                pe.wait_ge(y_ready, 1)
                pe.wait_ge(z_ready, GROUPS * CHUNKS)
                for m in range(H1 // 128):
                    block = slice(128 * m, 128 * m + 128)
                    pe.matmul(TAIL1[m], wt1[:, 0, block], s1[:, rows], start=True, stop=False)
                    pe.matmul(TAIL1[m], wt1_dense_parts[:, block], dense_parts[:, rows], start=False, stop=False)
                pe.wait_ge(s2_ready, CHUNKS)
                for m in range(H1 // 128):
                    pe.matmul(TAIL1[m], wt1[:, 1, 128 * m:128 * m + 128], s2[:, rows], start=False, stop=True)\
                        .then_inc(tail_done, 1)
                for k in range(H1 // 128):
                    pe.wait_ge(tail_vec if k % 2 else tail_act, k // 2 + 1)
                    for m in range(H2 // 128):
                        mm = pe.matmul(TAIL2[m], wt2[:, k, 128 * m:128 * m + 128], h1[:, k, rows],
                                       start=(k == 0), stop=(k == H1 // 128 - 1))
                        if k == H1 // 128 - 1:
                            mm.then_inc(tail_done, 1)
                pe.wait_ge(tail_act, 3)
                pe.matmul(TAIL3, wt3[:, 0:1], h2[:, 0, rows], start=True, stop=False)
                pe.wait_ge(tail_vec, 3)
                pe.matmul(TAIL3, wt3[:, 1:2], h2[:, 1, rows], start=False, stop=True).then_inc(tail_done, 1)

            pe.wait_ge(w1_hi_ready, 1)
            for _ in range(WARM_UP):
                pe.matmul(acc2[:, 0, :], w1_hi[:, 0, :], w1_hi[:, 0:COLS // N, :].rearrange("p t n -> p (t n)"),
                          start=True, stop=True)
            pe.wait_ge(w0_summed, 5)
            pe.wait_ge(w016_lo_ready, 2)
            layer1(0)
            pe.wait_ge(w1_full_in, 16)

            def step(c, i, p):
                wait_count(pe, v_ready, c - 1)
                first, last = isinstance(c, int) and c == 0, isinstance(c, int) and c == CHUNKS - 1
                if last:
                    pe.wait_ge(tower_in, 16 * 5)
                    pe.wait_ge(s2_ready, CHUNKS - 2)
                    pe.wait_ge(s1_ready, CHUNKS)
                for g in range(GROUPS):
                    group(c, g, p)
                    if g == AT_L1[first] and exists(c, 1):
                        layer1(c + 1)
                    if last and g < U:
                        unit(g)

            steps(pe, step)
            tail()


_TABLES = [f"tbl_{f}" for f in range(F)]


def kernel(**inputs):
    import concourse.bacc as bacc
    from concourse.bass_utils import run_bass_kernel_spmd

    tables = np.concatenate([np.asarray(inputs[t]) for t in _TABLES], axis=0)
    sizes = [np.asarray(inputs[t]).shape[0] for t in _TABLES]
    starts = np.array([sum(sizes[:f]) for f in range(F)], np.int32)
    ids = np.asarray(inputs["ids"]).T.reshape(F, CHUNKS, 4, GATHERS).transpose(0, 2, 1, 3).reshape(128, -1)
    row_base = np.broadcast_to(starts[:, None, None], (F, 4, CHUNKS * GATHERS)).reshape(128, -1).astype(ids.dtype)
    w0 = np.asarray(inputs["L0_rec_filter_0"])[0].reshape(F, F, N)
    h = np.arange(F)
    first = np.tile(h[None, :, None], (4, 1, 4))
    other = (first + 4 * np.arange(4)[:, None, None] + np.arange(4)) % F
    half = np.arange(WRAP)
    pad = lambda a: np.tile(np.concatenate([a, np.zeros_like(a)]), (4, 1))
    w1 = np.asarray(inputs["L0_rec_filter_1"])[0].reshape(4, GROUPS, 4, 32, N)
    q, r, g, j = np.ogrid[0:4, 0:32, 0:GROUPS, 0:SUB]
    w1 = w1[q, g, (q + j) % 4, r].reshape(128, GROUPS * SUB, N)[:, [SUB * g + j for g, j in TILES_SPLIT + TILES_WHOLE]]
    columns = lambda a, n: np.asarray(a).reshape(n, 128).T
    arrays = {
        "tables": tables,
        "ids": np.stack([ids, row_base], axis=1),
        "dense_t": pad(np.asarray(inputs["dense_ctx"]).T),
        "w0_a": w0[first, other].reshape(128, 4, N),
        "w0_b": w0[other, first].reshape(128, 4, N),
        "w0_a16": pad(w0[half, half + WRAP]),
        "w0_b16": pad(w0[half + WRAP, half]),
        "w1": w1,
        "w_top1": np.asarray(inputs["W_top1"])[:2 * N],
        "w_top1_dense": pad(np.asarray(inputs["W_top1"])[2 * N:]),
        "b_top1": columns(inputs["b_top1"], H1 // 128),
        "w_top2": np.asarray(inputs["W_top2"]),
        "b_top2": columns(inputs["b_top2"], H2 // 128),
        "w_top3": columns(inputs["W_top3"], H2 // 128),
    }
    arrays = {name: np.ascontiguousarray(a) for name, a in arrays.items()}
    nc = bacc.Bacc("TRN2", target_bir_lowering=False, num_devices=1)
    args = {name: nc.dram_tensor(name, a.shape, mybir.dt.from_np(a.dtype), kind="ExternalInput").ap()
            for name, a in arrays.items()}
    out = nc.dram_tensor("out", (B, 1), F32, kind="ExternalOutput").ap()
    build_cin_tower(nc, **args, out=out)
    return run_bass_kernel_spmd(nc, [arrays], core_ids=[0]).results[0]["out"]
```
